# Optimizing a Trainium2 kernel written in Bass

```python
import numpy as np
import jax
import jax.numpy as jnp

def _softmax(x, axis=-1):
    return jax.nn.softmax(x, axis=axis)

def _gelu(x):
    return jax.nn.gelu(x, approximate=True)

def _silu(x):
    return jax.nn.silu(x)

def _sigmoid(x):
    return jax.nn.sigmoid(x)

def _layernorm(x, axis=-1, eps=1e-05):
    m = jnp.mean(x, axis=axis, keepdims=True)
    v = jnp.var(x, axis=axis, keepdims=True)
    return (x - m) / jnp.sqrt(v + eps)

def _scatter_add(tgt, idx, src, axis=0):
    return tgt.at[idx].add(src)

def _segment_sum(src, seg, n):
    return jax.ops.segment_sum(src, seg, n)
kernel_name = 'mk_gnn_preln_d2_gnn_r8_c03c21'

def setup_inputs(seed: int=0):
    np.random.seed(seed)
    _w = jnp.asarray

    def _rec_inputs():
        import jax
        import jax.numpy as jnp
        _gk = jax.random.key(seed)
        x = -0.000202 + 1 * jax.random.normal(jax.random.fold_in(_gk, 1), (50000, 16), jnp.float32)
        _s = jax.random.randint(jax.random.fold_in(_gk, 2), (400000,), 0, 50000, jnp.int32)
        _d = jax.random.randint(jax.random.fold_in(_gk, 3), (400000,), 0, 50000, jnp.int32)
        _loop = jnp.arange(50000, dtype=jnp.int32)
        src = jnp.concatenate([_s, _d, _loop])
        dst = jnp.concatenate([_d, _s, _loop])
        _o = jnp.argsort(dst, stable=True)
        src = src[_o]
        dst = dst[_o]
        edge_attr_3 = -1.09012e-05 + 0.99985 * jax.random.normal(jax.random.fold_in(_gk, 12), (850000, 3), jnp.float32)
        edge_attr_48 = -3.69585e-06 + 0.999911 * jax.random.normal(jax.random.fold_in(_gk, 13), (850000, 48), jnp.float32)
        edge_type_6 = jax.random.randint(jax.random.fold_in(_gk, 15), (850000,), 0, 6, jnp.int32)
        return (x, src, dst, edge_attr_3, edge_attr_48, edge_type_6)
    x, src, dst, edge_attr_3, edge_attr_48, edge_type_6 = _rec_inputs()

    def _L0_gnn_setup():
        import jax, jax.numpy as jnp
        import numpy as np
        N = 6250
        E_RAND = 200000
        IN = 8
        OUT = 8
        B = 16
        T = 5
        key = jax.random.key(seed)
        k1, k2, k3, k4, k5, k6 = jax.random.split(key, 6)
        x = jax.random.normal(k1, (N * IN, B), jnp.float32)
        loops = jnp.arange(N, dtype=jnp.int32)
        src = jnp.concatenate([loops, jax.random.randint(k2, (E_RAND,), 0, N, jnp.int32)])
        dst = jnp.concatenate([loops, jax.random.randint(k3, (E_RAND,), 0, N, jnp.int32)])
        edge_types = jnp.concatenate([jnp.ones(N, jnp.int32), jax.random.randint(k4, (E_RAND,), 2, T + 1, jnp.int32)])
        bound = 1.0 / np.sqrt(IN)
        W = jax.random.uniform(k5, (T, OUT, IN), jnp.float32, -bound, bound)
        Bv = jax.random.uniform(k6, (T, OUT), jnp.float32, -bound, bound)
        return dict(x=x, W=W, Bv=Bv, src=src, dst=dst, edge_types=edge_types)
    _L0_gnn_all = _L0_gnn_setup()
    _L0_gnn_in = {k: v for k, v in _L0_gnn_all.items() if k in ('W', 'Bv')}
    del _L0_gnn_all

    def _L1_gnn_setup():
        import jax, jax.numpy as jnp
        import numpy as np
        NS, NV = (16, 4)
        EPS = 1e-05
        N_NODES, N_EDGES = (5000, 50000)

        def _bn_scalar(x, g, b):
            m = x.mean(0)
            v = ((x - m) ** 2).mean(0)
            return (x - m) / jnp.sqrt(v + EPS) * g + b

        def _seg_mean(x, idx, n):
            s = jax.ops.segment_sum(x, idx, num_segments=n)
            c = jax.ops.segment_sum(jnp.ones((idx.shape[0],), x.dtype), idx, num_segments=n)
            return s / jnp.maximum(c, 1.0)[:, None]

        def _edge_weights(edge_attr, w1, b1, w2, b2):
            h = jax.nn.relu(edge_attr @ w1 + b1)
            return h @ w2 + b2

        def _forward(node_attr, edge_attr, edge_vec, fc0_w1, fc0_b1, fc0_w2, fc0_b2, fc1_w1, fc1_b1, fc1_w2, fc1_b2, bn0_gs, bn0_bs, bn0_gv, bn1_gs, bn1_bs, edge_index):
            N = node_attr.shape[0]
            E = edge_attr.shape[0]
            src, dst = (edge_index[0], edge_index[1])
            rhat = edge_vec / (jnp.linalg.norm(edge_vec, axis=-1, keepdims=True) + 1e-12)
            sh1 = rhat * float(np.sqrt(3.0))
            w = _edge_weights(edge_attr, fc0_w1, fc0_b1, fc0_w2, fc0_b2)
            wa = w[:, :NS * NS].reshape(E, NS, NS)
            wb = w[:, NS * NS:].reshape(E, NS, NV)
            x = node_attr[dst]
            inv = float(1.0 / np.sqrt(NS))
            msg_s = jnp.einsum('ei,eij->ej', x, wa) * inv
            msg_v = jnp.einsum('ei,eij,ec->ejc', x, wb, sh1) * inv
            msg = jnp.concatenate([msg_s, msg_v.reshape(E, NV * 3)], axis=-1)
            out = _seg_mean(msg, src, N)
            s0 = _bn_scalar(out[:, :NS], bn0_gs, bn0_bs)
            v0 = out[:, NS:].reshape(N, NV, 3)
            vn = jnp.sqrt((v0 ** 2).mean(axis=(0, 2)) + EPS)
            v0 = v0 / vn[None, :, None] * bn0_gv[None, :, None]
            w = _edge_weights(edge_attr, fc1_w1, fc1_b1, fc1_w2, fc1_b2)
            wa = w[:, :NS * NS].reshape(E, NS, NS)
            wb = w[:, NS * NS:].reshape(E, NV, NS)
            s = s0[dst]
            v = v0[dst]
            path_a = jnp.einsum('ei,eij->ej', s, wa)
            path_b = jnp.einsum('eic,ec,eij->ej', v, sh1, wb) * float(1.0 / np.sqrt(3.0))
            msg = (path_a + path_b) * float(1.0 / np.sqrt(NS + NV))
            node1 = _seg_mean(msg, src, N)
            return _bn_scalar(node1, bn1_gs, bn1_bs)
        key = jax.random.key(seed)
        ks = jax.random.split(key, 8)
        d = 3 * NS
        wn = NS * NS + NS * NV
        g = lambda k, shape, sc: jax.random.normal(k, shape, jnp.float32) * sc
        return {'node_attr': g(ks[0], (N_NODES, NS), 1.0), 'edge_attr': g(ks[1], (N_EDGES, d), 1.0), 'edge_vec': g(ks[2], (N_EDGES, 3), 1.0), 'fc0_w1': g(ks[3], (d, d), d ** (-0.5)), 'fc0_b1': jnp.zeros((d,), jnp.float32), 'fc0_w2': g(ks[4], (d, wn), d ** (-0.5)), 'fc0_b2': jnp.zeros((wn,), jnp.float32), 'fc1_w1': g(ks[5], (d, d), d ** (-0.5)), 'fc1_b1': jnp.zeros((d,), jnp.float32), 'fc1_w2': g(ks[6], (d, wn), d ** (-0.5)), 'fc1_b2': jnp.zeros((wn,), jnp.float32), 'bn0_gs': jnp.ones((NS,), jnp.float32), 'bn0_bs': jnp.zeros((NS,), jnp.float32), 'bn0_gv': jnp.ones((NV,), jnp.float32), 'bn1_gs': jnp.ones((NS,), jnp.float32), 'bn1_bs': jnp.zeros((NS,), jnp.float32), 'edge_index': jax.random.randint(ks[7], (2, N_EDGES), 0, N_NODES)}
    _L1_gnn_all = _L1_gnn_setup()
    _L1_gnn_in = {k: v for k, v in _L1_gnn_all.items() if k in ('fc0_w1', 'fc0_b1', 'fc0_w2', 'fc0_b2', 'fc1_w1', 'fc1_b1', 'fc1_w2', 'fc1_b2', 'bn0_gs', 'bn0_bs', 'bn0_gv', 'bn1_gs', 'bn1_bs')}
    del _L1_gnn_all
    return {'x': x, 'src': src, 'dst': dst, 'edge_attr_3': edge_attr_3, 'edge_attr_48': edge_attr_48, 'edge_type_6': edge_type_6, 'L0_gnn_W': _L0_gnn_in['W'], 'L0_gnn_Bv': _L0_gnn_in['Bv'], 'L1_gnn_fc0_w1': _L1_gnn_in['fc0_w1'], 'L1_gnn_fc0_b1': _L1_gnn_in['fc0_b1'], 'L1_gnn_fc0_w2': _L1_gnn_in['fc0_w2'], 'L1_gnn_fc0_b2': _L1_gnn_in['fc0_b2'], 'L1_gnn_fc1_w1': _L1_gnn_in['fc1_w1'], 'L1_gnn_fc1_b1': _L1_gnn_in['fc1_b1'], 'L1_gnn_fc1_w2': _L1_gnn_in['fc1_w2'], 'L1_gnn_fc1_b2': _L1_gnn_in['fc1_b2'], 'L1_gnn_bn0_gs': _L1_gnn_in['bn0_gs'], 'L1_gnn_bn0_bs': _L1_gnn_in['bn0_bs'], 'L1_gnn_bn0_gv': _L1_gnn_in['bn0_gv'], 'L1_gnn_bn1_gs': _L1_gnn_in['bn1_gs'], 'L1_gnn_bn1_bs': _L1_gnn_in['bn1_bs']}

def reference(x, src, dst, edge_attr_3, edge_attr_48, edge_type_6, L0_gnn_W, L0_gnn_Bv, L1_gnn_fc0_w1, L1_gnn_fc0_b1, L1_gnn_fc0_w2, L1_gnn_fc0_b2, L1_gnn_fc1_w1, L1_gnn_fc1_b1, L1_gnn_fc1_w2, L1_gnn_fc1_b2, L1_gnn_bn0_gs, L1_gnn_bn0_bs, L1_gnn_bn0_gv, L1_gnn_bn1_gs, L1_gnn_bn1_bs):
    import jax
    import jax.numpy as jnp

    def _L0_gnn_ref(x, W, Bv, src, dst, edge_types):
        import jax, jax.numpy as jnp
        import numpy as np
        N = 6250
        E_RAND = 200000
        IN = 8
        OUT = 8
        B = 16
        T = 5
        T_, OUT_, IN_ = W.shape
        Nn = x.shape[0] // IN_
        xr = x.reshape(Nn, IN_, -1)
        Wg = W[edge_types - 1]
        msg = jnp.einsum('eoi,eib->eob', Wg, xr[src])
        y = jax.ops.segment_sum(msg, dst, num_segments=Nn)
        yb = jax.ops.segment_sum(Bv[edge_types - 1], dst, num_segments=Nn)
        y = y + yb[:, :, None]
        return y.reshape(Nn * OUT_, -1)

    def _L1_gnn_ref(node_attr, edge_attr, edge_vec, fc0_w1, fc0_b1, fc0_w2, fc0_b2, fc1_w1, fc1_b1, fc1_w2, fc1_b2, bn0_gs, bn0_bs, bn0_gv, bn1_gs, bn1_bs, edge_index):
        import jax, jax.numpy as jnp
        import numpy as np
        NS, NV = (16, 4)
        EPS = 1e-05
        N_NODES, N_EDGES = (5000, 50000)

        def _bn_scalar(x, g, b):
            m = x.mean(0)
            v = ((x - m) ** 2).mean(0)
            return (x - m) / jnp.sqrt(v + EPS) * g + b

        def _seg_mean(x, idx, n):
            s = jax.ops.segment_sum(x, idx, num_segments=n)
            c = jax.ops.segment_sum(jnp.ones((idx.shape[0],), x.dtype), idx, num_segments=n)
            return s / jnp.maximum(c, 1.0)[:, None]

        def _edge_weights(edge_attr, w1, b1, w2, b2):
            h = jax.nn.relu(edge_attr @ w1 + b1)
            return h @ w2 + b2

        def _forward(node_attr, edge_attr, edge_vec, fc0_w1, fc0_b1, fc0_w2, fc0_b2, fc1_w1, fc1_b1, fc1_w2, fc1_b2, bn0_gs, bn0_bs, bn0_gv, bn1_gs, bn1_bs, edge_index):
            N = node_attr.shape[0]
            E = edge_attr.shape[0]
            src, dst = (edge_index[0], edge_index[1])
            rhat = edge_vec / (jnp.linalg.norm(edge_vec, axis=-1, keepdims=True) + 1e-12)
            sh1 = rhat * float(np.sqrt(3.0))
            w = _edge_weights(edge_attr, fc0_w1, fc0_b1, fc0_w2, fc0_b2)
            wa = w[:, :NS * NS].reshape(E, NS, NS)
            wb = w[:, NS * NS:].reshape(E, NS, NV)
            x = node_attr[dst]
            inv = float(1.0 / np.sqrt(NS))
            msg_s = jnp.einsum('ei,eij->ej', x, wa) * inv
            msg_v = jnp.einsum('ei,eij,ec->ejc', x, wb, sh1) * inv
            msg = jnp.concatenate([msg_s, msg_v.reshape(E, NV * 3)], axis=-1)
            out = _seg_mean(msg, src, N)
            s0 = _bn_scalar(out[:, :NS], bn0_gs, bn0_bs)
            v0 = out[:, NS:].reshape(N, NV, 3)
            vn = jnp.sqrt((v0 ** 2).mean(axis=(0, 2)) + EPS)
            v0 = v0 / vn[None, :, None] * bn0_gv[None, :, None]
            w = _edge_weights(edge_attr, fc1_w1, fc1_b1, fc1_w2, fc1_b2)
            wa = w[:, :NS * NS].reshape(E, NS, NS)
            wb = w[:, NS * NS:].reshape(E, NV, NS)
            s = s0[dst]
            v = v0[dst]
            path_a = jnp.einsum('ei,eij->ej', s, wa)
            path_b = jnp.einsum('eic,ec,eij->ej', v, sh1, wb) * float(1.0 / np.sqrt(3.0))
            msg = (path_a + path_b) * float(1.0 / np.sqrt(NS + NV))
            node1 = _seg_mean(msg, src, N)
            return _bn_scalar(node1, bn1_gs, bn1_bs)
        return _forward(node_attr, edge_attr, edge_vec, fc0_w1, fc0_b1, fc0_w2, fc0_b2, fc1_w1, fc1_b1, fc1_w2, fc1_b2, bn0_gs, bn0_bs, bn0_gv, bn1_gs, bn1_bs, edge_index)
    edge_index = jnp.stack([src, dst])
    h = jnp.maximum(_layernorm(x, axis=-1), 0.0)
    x = x + _L0_gnn_ref(h, L0_gnn_W, L0_gnn_Bv, src, dst, edge_type_6)
    h = jnp.maximum(_layernorm(x, axis=-1), 0.0)
    x = x + _L1_gnn_ref(h, edge_attr_48, edge_attr_3, L1_gnn_fc0_w1, L1_gnn_fc0_b1, L1_gnn_fc0_w2, L1_gnn_fc0_b2, L1_gnn_fc1_w1, L1_gnn_fc1_b1, L1_gnn_fc1_w2, L1_gnn_fc1_b2, L1_gnn_bn0_gs, L1_gnn_bn0_bs, L1_gnn_bn0_gv, L1_gnn_bn1_gs, L1_gnn_bn1_bs, edge_index)
    return x

_drawn_inputs = setup_inputs


def setup_inputs(seed=0):
    import zlib

    import numpy as np

    out = dict(_drawn_inputs(seed))
    spreads = {'L1_gnn_fc0_b1': (0.0, 0.329),
     'L1_gnn_fc0_b2': (0.0, 0.1),
     'L1_gnn_fc1_b1': (0.0, 0.1),
     'L1_gnn_fc1_b2': (0.0, 0.1),
     'L1_gnn_bn0_gs': (1.0, 0.2),
     'L1_gnn_bn0_bs': (0.0, 0.401),
     'L1_gnn_bn0_gv': (1.0, 0.6),
     'L1_gnn_bn1_gs': (1.0, 0.2),
     'L1_gnn_bn1_bs': (0.0, 0.301)}
    factors = {}
    for name, (base, spread) in spreads.items():
        noise = np.random.default_rng([zlib.crc32(name.encode()), seed]).standard_normal(out[name].shape)
        drawn = base * np.exp(spread * noise) if base else spread * noise
        out[name] = jnp.asarray(drawn.astype(out[name].dtype))
    for name, factor in factors.items():
        out[name] = (out[name] * factor).astype(out[name].dtype)
    return out
```

```python
from contextlib import ExitStack

import numpy as np
import concourse.bass as bass
from concourse import mybir

F32 = mybir.dt.float32
I32 = mybir.dt.int32
ALU = mybir.AluOpType
ACT = mybir.ActivationFunctionType
AX = mybir.AxisListType.X
RMAX = bass.bass_isa.ReduceOp.max

P = 128
TPG = 8
GPT = 4
EPG = P * TPG
REPL = 4
EPS = 1e-5
NS, NV, SH = 16, 4, 3
H = 48
WN = NS * NS + NS * NV
NT = 5
L0 = 8 * NS
ROW_A = 32
ROW_B = NS
COLS_A = 34
COLS_B = NS + 1
TAB = NV * SH + NS
PIECES = 8


def build(nc, N, NG, x, src_cols, dst_cols, typ_cols, vec_cols, src_row, dst_row, attr, turn_no,
          ident, code, spare, node_mask, copy_mask, w_l0, b_l0, w1, b1, w2a, w2b,
          gs0, bs0, gv0, gs1, bs1, out):
    K = x.shape[1] // NS
    NP = P * K
    N0 = N // 8
    K0 = K // 8
    NP0 = P * K0
    TT = NG * TPG
    TURNS = NG // GPT
    PG = NG // PIECES
    XW = K * NS

    def dram(name, shape, dt=F32):
        return nc.dram_tensor(name, shape, dt, kind="Internal").ap()

    z_tab = dram("z_tab", (NP0 * NT, L0))
    z_idx = dram("z_idx", (P, TT), I32)
    side0 = dram("side0", (P, NG * 2 * TPG))
    side = dram("side", (P, NG * 4 * TPG))
    h_tab = dram("h_tab", (NP, NS))
    s_tab = dram("s_tab", (NP, TAB))
    acc0 = [dram(f"acc0_{r}", (NP0 + P, L0)) for r in range(REPL)]
    accA = [dram(f"accA_{r}", (NP + P, ROW_A)) for r in range(REPL)]
    accB = [dram(f"accB_{r}", (NP + P, ROW_B)) for r in range(REPL)]

    with ExitStack() as ctx:
        def sb(name, shape, dt=F32):
            return ctx.enter_context(nc.sbuf_tensor(name, shape, dt))

        def sem(name):
            return ctx.enter_context(nc.semaphore(name))

        xs = sb("xs", [P, XW])
        T = sb("T", [P, K * TAB])
        rcount = sb("rcount", [P, K])
        mask = sb("mask", [P, K])
        small = sb("small", [P, 4, K])
        ident_sb = sb("ident_sb", [P, P])
        ones = sb("ones", [P, P])
        code_sb = sb("code_sb", [P, 2])
        spare0 = sb("spare0", [P, 2])
        cmask = sb("cmask", [P, NS])
        wl = sb("wl", [P, NT * 8])
        bl = sb("bl", [P, NT * 8])
        Mk = sb("Mk", [P, NT * L0])
        w1_sb = [sb(f"w1_{r}", [H, P]) for r in range(2)]
        b1_sb = [sb(f"b1_{r}", [H, 1]) for r in range(2)]
        w2_sb = [sb(f"w2_{r}", [H + 1, WN]) for r in range(2)]
        bn = sb("bn", [P, 5 * NS])
        stat = sb("stat", [P, 8, 32])
        vmax = sb("vmax", [P, 2])
        turns_sb = sb("turns_sb", [P, 1], I32)
        zero = sb("zero", [P, 2048])
        ARENA = max(20480, 4 * XW // 4 + 3 * XW)
        arena = sb("arena", [P, ARENA])

        def carve(sizes):
            views, at = [], 0
            for n in sizes:
                views.append(arena[:, at:at + n])
                at += n
            assert at <= ARENA, at
            return views

        banks = [ctx.enter_context(nc.psum_tensor(f"bank{i}", [P, 512], F32)) for i in range(4)]
        wide = [ctx.enter_context(nc.psum_tensor(f"wide{i}", [P, 2, 512], F32)) for i in range(2)]

        ld_const = sem("ld_const")
        zeroed = sem("zeroed")
        zero_set = sem("zero_set")
        c = sem("dve_step")
        chain = [0]
        sqrt_in = sem("sqrt_in")
        sqrt_out = sem("sqrt_out")
        nsq = [0]

        block = ctx.enter_context(nc.Block())

        def k16(t):
            return t.rearrange("p (k c) -> p k c", c=NS)

        def per_node(v, w):
            return v.unsqueeze(2).broadcast_to([P, K, w])

        def per_chan(v, w):
            return v.unsqueeze(1).broadcast_to([P, K, w])

        def link(ins):
            chain[0] += 1
            ins.then_inc(c, 1)
            nc.vector.wait_ge(c, chain[0])

        def dve_sqrt(ap):
            nsq[0] += 1
            nc.vector.sem_inc(sqrt_in, 1)
            nc.vector.wait_ge(sqrt_out, nsq[0])

        x_in = sem("x_in")
        h0_done = sem("h0_done")
        zT_done, zTc_done, z_mm, z_sum, z_out = (sem(s) for s in ("zT_done", "zTc_done", "z_mm", "z_sum", "z_out"))
        pc_in, pc_done, pc_out = sem("pc_in"), sem("pc_done"), sem("pc_out")
        pc_sq, pc_root = sem("pc_sq"), sem("pc_root")
        psem, qsem = sem("pc_step"), sem("pc_tail")
        bound_in, bound_red, bound_out = sem("bound_in"), sem("bound_red"), sem("bound_out")
        l0_done = sem("l0_done")
        paced, zh_done = sem("paced"), sem("zh_done")
        y_in, y_used = sem("y_in"), sem("y_used")
        h1_done, h1_out = sem("h1_done"), sem("h1_out")
        rA_done, rB_done = sem("rA_done"), sem("rB_done")
        t_in = [sem("tA_in"), sem("tB_in")]
        t_used = [sem("tA_used"), sem("tB_used")]
        part_in, part_sum = sem("part_in"), sem("part_sum")
        s_done, s_out = sem("s_done"), sem("s_out")
        fin, fin_out = sem("fin"), sem("fin_out")

        h_p, d_p, zTs, zh, zts = carve([XW, XW, P, P, NT * L0])
        used = 2 * XW + P + NT * L0
        W8 = PG * TPG
        at = [0]
        srcp, dstp, typp, vecp, shp, rootp, t1p, t2p, sidep, side0p, zip_, turnp = carve(
            [W8, W8, W8, 3 * W8, 3 * W8, W8, W8, W8, 4 * W8, 2 * W8, W8, PG])
        srcp, dstp, typp, zip_i = srcp.bitcast(I32), dstp.bitcast(I32), typp.bitcast(I32), zip_.bitcast(I32)

        v = carve([GPT * EPG, GPT * TPG * (L0 + 1), GPT * TPG * L0, 2 * EPG, GPT * TPG, GPT * 2 * TPG, GPT * TPG, TPG])
        rowb0 = v[0].bitcast(I32).rearrange("p (s e) -> p s e", s=GPT)
        zb = v[1].rearrange("p (s t c) -> p s t c", s=GPT, t=TPG)
        out0 = v[2].rearrange("p (s t c) -> p s t c", s=GPT, t=TPG)
        S0 = v[3].rearrange("p (s e) -> p s e", s=2)
        zi = v[4].bitcast(I32).rearrange("p (s t) -> p s t", s=GPT)
        sd0 = v[5].rearrange("p (s t) -> p s t", s=GPT)
        ui0 = v[6].bitcast(I32).rearrange("p (s t) -> p s t", s=GPT)
        tmp0 = v[7]

        v = carve([GPT * EPG, GPT * EPG, GPT * TPG * 32, 2 * 2 * WN, 2 * EPG, 2 * EPG, 2 * TPG * COLS_A,
                   GPT * TPG * ROW_A, GPT * TPG, GPT * 4 * TPG, GPT * TPG, 2 * TPG, TPG * NV * SH])
        rowb = v[0].bitcast(I32).rearrange("p (s e) -> p s e", s=GPT)
        ea = v[1].rearrange("p (s e) -> p s e", s=GPT)
        xg = v[2].rearrange("p (s t c) -> p s t c", s=GPT, t=TPG)
        prod = v[3].rearrange("p (s t w) -> p s t w", s=2, t=2)
        Sm = v[4].rearrange("p (s e) -> p s e", s=2)
        hT = v[5].rearrange("p (s e) -> p s e", s=2)
        Mflat = v[6]
        outflat = v[7]
        di = v[8].bitcast(I32).rearrange("p (s t) -> p s t", s=GPT)
        sd = v[9].rearrange("p (s t) -> p s t", s=GPT)
        ui = v[10].bitcast(I32).rearrange("p (s t) -> p s t", s=GPT)
        away = v[11].rearrange("p (s t) -> p s t", s=2)
        vtmp = v[12].rearrange("p (t j c) -> p t j c", j=NV, c=SH)

        y_st = carve([XW] * REPL)
        TP = 4
        KP = K // TP
        stA = carve([KP * ROW_A] * REPL)
        stB = carve([KP * ROW_B] * REPL)
        sqT = carve([K * TAB])[0]
        nb = carve([XW, XW])

        class EdgeLoop:

            def __init__(r, name, n):
                r.n = n
                r.ld_idx = [sem(f"{name}_idx{s}") for s in range(GPT)]
                r.ld_rest = [sem(f"{name}_rest{s}") for s in range(GPT)]
                r.rest = 16 * (3 if n else 2)
                r.gathered = [sem(f"{name}_gathered{s}") for s in range(GPT)]
                r.summed = [sem(f"{name}_summed{q}") for q in range(REPL)]
                r.inputs_free = sem(name + "_inputs_free")
                r.x_free = sem(name + "_x_free")
                r.out_free = sem(name + "_out_free")
                r.S_built = sem(name + "_S_built")
                r.joined = sem(name + "_joined")
                r.out_ready = sem(name + "_out_ready")
                r.idx_ready = sem(name + "_idx_ready")
                r.set_up = sem(name + "_set_up")
                r.step = sem(name + "_step")
                if n == 0:
                    return
                r.hid = sem(name + "_hid")
                r.relu = sem(name + "_relu")
                r.weights = sem(name + "_weights")
                r.prod = sem(name + "_prod")
                r.red = sem(name + "_red")
                r.vec = sem(name + "_vec")
                r.msgs = sem(name + "_msgs")

        R0, RA, RB = EdgeLoop("l0", 0), EdgeLoop("a", 1), EdgeLoop("b", 2)

        @block.sync
        def _(sp):
            sp.dma_start(xs[:, :], x).then_inc(x_in, 16)
            n = 0
            for dst_, src_ in ((ident_sb[:, :], ident), (code_sb[:, :], code), (spare0[:, :], spare),
                               (mask[:, :], node_mask), (cmask[:, :], copy_mask), (wl[:, :], w_l0),
                               (bl[:, :], b_l0.partition_broadcast(P)), (w1_sb[0][:, :], w1[0]),
                               (w1_sb[1][:, :], w1[1]), (b1_sb[0][:, :], b1[0]), (b1_sb[1][:, :], b1[1]),
                               (w2_sb[0][:, :], w2a), (w2_sb[1][:, :], w2b),
                               (bn[:, 0:NS], gs0.partition_broadcast(P)), (bn[:, NS:2 * NS], bs0.partition_broadcast(P)),
                               (bn[:, 2 * NS:3 * NS], gs1.partition_broadcast(P)),
                               (bn[:, 3 * NS:4 * NS], bs1.partition_broadcast(P)),
                               (bn[:, 4 * NS:4 * NS + NV], gv0.partition_broadcast(P))):
                sp.dma_start(dst_, src_).then_inc(ld_const, 16)
                n += 1
            assert n == NCONST

            z_rows = z_tab.rearrange("(p k t) c -> p k (t c)", p=P, t=NT)
            with sp.Fori(0, K0) as k:
                sp.wait_ge(z_sum, 2 * k + 2)
                sp.dma_start(z_rows[:, bass.ds(k, 1), :].rearrange("p a c -> p (a c)"), zts).then_inc(z_out, 16)

            with sp.Fori(0, PIECES) as q:
                sp.wait_ge(pc_out, 48 * q)
                sp.wait_ge(z_out, 16 * K0)
                sp.dma_start(srcp, src_cols[:, bass.ds(q * W8, W8)]).then_inc(pc_in, 16)
                sp.dma_start(dstp, dst_cols[:, bass.ds(q * W8, W8)]).then_inc(pc_in, 16)
                sp.dma_start(typp, typ_cols[:, bass.ds(q * W8, W8)]).then_inc(pc_in, 16)
                sp.dma_start(vecp, vec_cols[:, bass.ds(q * 3 * W8, 3 * W8)]).then_inc(pc_in, 16)
                sp.dma_start(turnp, turn_no[:, bass.ds(q * PG, PG)]).then_inc(pc_in, 16)
                sp.wait_ge(pc_done, q + 1)
                sp.dma_start(side[:, bass.ds(q * 4 * W8, 4 * W8)], sidep).then_inc(pc_out, 16)
                sp.dma_start(side0[:, bass.ds(q * 2 * W8, 2 * W8)], side0p).then_inc(pc_out, 16)
                sp.dma_start(z_idx[:, bass.ds(q * W8, W8)], zip_i).then_inc(pc_out, 16)
            sp.wait_ge(pc_out, 48 * PIECES)

            sp.wait_ge(bound_out, 1)
            turns = sp.value_load(turns_sb[0:1, 0:1], min_val=1, max_val=TURNS)
            with sp.Fori(0, turns) as it:
                for s in range(GPT):
                    g = it * GPT + s
                    sp.wait_ge(R0.inputs_free, g + 1)
                    sp.dma_start(zi[:, s, :], z_idx[:, bass.ds(g * TPG, TPG)]).then_inc(R0.ld_idx[s], 16)
                    sp.dma_start(sd0[:, s, :], side0[:, bass.ds(g * 2 * TPG, 2 * TPG)]).then_inc(R0.ld_rest[s], 16)
                    sp.dma_start(rowb0[:, s, :], dst_row[bass.ds(g * EPG, EPG)].partition_broadcast(P)).then_inc(R0.ld_rest[s], 16)

            sp.wait_ge(l0_done, 1)
            for r in range(REPL):
                sp.dma_start(y_st[r], acc0[r][0:NP0, :].rearrange("(p k) c -> p (k c)", p=P)).then_inc(y_in, 16)
            sp.wait_ge(h1_done, 1)
            sp.dma_start(h_tab.rearrange("(p k) c -> p (k c)", p=P), nb[0]).then_inc(h1_out, 16)
            sp.wait_ge(h1_out, 16)

            def feed(R):
                with sp.Fori(0, TURNS) as it:
                    for s in range(GPT):
                        g = it * GPT + s
                        sp.wait_ge(R.inputs_free, g + 1)
                        sp.dma_start(di[:, s, :], dst_cols[:, bass.ds(g * TPG, TPG)]).then_inc(R.ld_idx[s], 16)
                        sp.dma_start(ea[0:H, s, :], attr[:, bass.ds(g * EPG, EPG)]).then_inc(R.ld_rest[s], 16)
                        sp.dma_start(rowb[:, s, :], src_row[bass.ds(g * EPG, EPG)].partition_broadcast(P)).then_inc(R.ld_rest[s], 16)
                        sp.dma_start(sd[:, s, :], side[:, bass.ds(g * 4 * TPG, 4 * TPG)]).then_inc(R.ld_rest[s], 16)

            def tables(R, acc, st, row, n):
                for q in range(TP):
                    if q:
                        sp.wait_ge(t_used[n], q)
                    for r in range(REPL):
                        sp.dma_start(st[r], acc[r][0:NP, :].rearrange("(p k) c -> p (k c)", p=P)
                                     [:, q * KP * row:(q + 1) * KP * row]).then_inc(t_in[n], 16)

            feed(RA)
            sp.wait_ge(rA_done, 1)
            tables(RA, accA, stA, ROW_A, 0)
            sp.wait_ge(s_done, 1)
            sp.dma_start(s_tab.rearrange("(p k) c -> p (k c)", p=P), T[:, :]).then_inc(s_out, 16)
            sp.wait_ge(s_out, 16)
            feed(RB)
            sp.wait_ge(rB_done, 1)
            tables(RB, accB, stB, ROW_B, 1)
            sp.wait_ge(fin, 1)
            sp.dma_start(out, xs[:, :]).then_inc(fin_out, 16)
            sp.wait_ge(fin_out, 16)

        @block.gpsimd
        def _(pool):
            last_row = {rows: pool.to_reg(rows - 1) for rows in sorted({NP0 * NT, NP, NP0 + P, NP + P})}

            def gather(dst_, tab, idx, signal):
                pool.indirect_dma_start(out=dst_, out_offset=None, in_=tab,
                                        in_offset=bass.IndirectOffsetOnAxis(ap=idx, axis=0),
                                        bounds_check=last_row[tab.shape[0]], oob_is_err=True).then_inc(signal, 16)

            def add_rows(tab, src_, idx, signal):
                pool.indirect_dma_start(out=tab, out_offset=bass.IndirectOffsetOnAxis(ap=idx, axis=0),
                                        in_=src_, in_offset=None, bounds_check=last_row[tab.shape[0]],
                                        oob_is_err=True, compute_op=ALU.add).then_inc(signal, 16)

            pool.wait_ge(zero_set, 1)
            n = 0
            for acc in acc0 + accA + accB:
                flat = acc.rearrange("(p k) c -> p (k c)", p=P)
                w = flat.shape[1]
                for a in range(0, w, 2048):
                    b = min(w, a + 2048)
                    pool.dma_start(flat[:, a:b], zero[:, 0:b - a]).then_inc(zeroed, 16)
                    n += 1
            pool.wait_ge(zeroed, 16 * n)

            pool.wait_ge(bound_in, 1)
            pool.partition_all_reduce(vmax[:, 1:2], vmax[:, 0:1], P, RMAX).then_inc(bound_red, 1)
            pool.wait_ge(bound_red, 1)
            pool.tensor_copy(turns_sb[:, :], vmax[:, 1:2]).then_inc(bound_out, 1)
            pool.wait_ge(bound_out, 1)
            turns = pool.value_load(turns_sb[0:1, 0:1], min_val=1, max_val=TURNS)

            R = R0
            pool.wait_ge(z_out, 16 * K0)
            pool.sem_inc(R.out_free, GPT - 1)
            with pool.Fori(0, turns) as it:
                for s in range(GPT):
                    g = it * GPT + s
                    pool.wait_ge(R.ld_idx[s], 16 * it + 16)
                    pool.wait_ge(R.x_free, g + 1)
                    pool.sem_inc(paced, 1)
                    for t in range(TPG):
                        gather(zb[:, s, t, 0:L0], z_tab, zi[:, s, t:t + 1], R.gathered[s])
                    pool.wait_ge(R.out_ready, g + 1)
                    pool.wait_ge(R.idx_ready, g + 1)
                    for t in range(TPG):
                        pool.wait_ge(R.summed[t % REPL], 16 * (TPG // REPL) * g + 16 * (t // REPL))
                        pool.sem_inc(paced, 1)
                        add_rows(acc0[t % REPL], out0[:, s, t, :], ui0[:, s, t:t + 1], R.summed[t % REPL])
                    pool.sem_inc(R.out_free, 1)
            for r in range(REPL):
                pool.wait_ge(R.summed[r], 16 * (TPG // REPL) * GPT * turns)
            pool.sem_inc(l0_done, 1)

            def edges(R, tab, width, acc, row, xcols):
                outv = outflat.rearrange("p (s t c) -> p s t c", s=GPT, t=TPG)[:, :, :, 0:row]

                def fetch(s, t):
                    gather(xg[:, s, t, xcols:xcols + width], tab, di[:, s, t:t + 1], R.gathered[s])

                def fetch_waits(g, s, turn):
                    pool.wait_ge(R.ld_idx[s], 16 * turn + 16)
                    pool.wait_ge(R.x_free, g + 1)
                    pool.sem_inc(paced, 1)

                def body(it, last):
                    for s in range(GPT):
                        g = it * GPT + s
                        ahead = (s + 2) % GPT
                        more = not (last and s + 2 >= GPT)
                        if more:
                            fetch_waits(g + 2, ahead, it + (s + 2) // GPT)
                            for t in range(TPG // 2):
                                fetch(ahead, t)
                        pool.wait_ge(R.out_ready, g + 1)
                        pool.wait_ge(R.idx_ready, g + 1)
                        for t in range(TPG):
                            pool.wait_ge(R.summed[t % REPL], 16 * (TPG // REPL) * g + 16 * (t // REPL))
                            pool.sem_inc(paced, 1)
                            add_rows(acc[t % REPL], outv[:, s, t, :], ui[:, s, t:t + 1], R.summed[t % REPL])
                            if more and t % 2:
                                fetch(ahead, TPG // 2 + t // 2)
                        pool.sem_inc(R.out_free, 1)

                pool.sem_inc(R.out_free, GPT - 1)
                for g in range(2):
                    fetch_waits(g, g, 0)
                    for t in range(TPG):
                        fetch(g, t)
                with pool.Fori(0, TURNS - 1) as it:
                    body(it, False)
                body(TURNS - 1, True)
                for r in range(REPL):
                    pool.wait_ge(R.summed[r], 16 * (TPG // REPL) * NG)

            pool.wait_ge(h1_out, 16)
            edges(RA, h_tab, NS, accA, ROW_A, 12)
            pool.sem_inc(rA_done, 1)
            pool.wait_ge(s_out, 16)
            edges(RB, s_tab, TAB, accB, ROW_B, 0)
            pool.sem_inc(rB_done, 1)

        @block.tensor
        def _(pe):
            pe.wait_ge(h0_done, 1)
            pe.wait_ge(ld_const, 16 * NCONST)
            with pe.Fori(0, K0) as k:
                pe.wait_ge(zTc_done, k)
                pe.wait_ge(zh_done, k + 1)
                pe.transpose(banks[0][:, 0:P], zh, ident_sb[:, :]).then_inc(zT_done, 1)
                pe.wait_ge(zTc_done, k + 1)
                pe.wait_ge(z_sum, 2 * k)
                pe.matmul(banks[1][:, 0:NT * L0 // 2], zTs, Mk[:, 0:NT * L0 // 2], start=True, stop=True).then_inc(z_mm, 1)
                pe.matmul(banks[2][:, 0:NT * L0 // 2], zTs, Mk[:, NT * L0 // 2:], start=True, stop=True).then_inc(z_mm, 1)

            pe.wait_ge(bound_out, 1)
            turns = pe.value_load(turns_sb[0:1, 0:1], min_val=1, max_val=TURNS)
            R = R0
            with pe.Fori(0, turns) as it:
                for s in range(GPT):
                    g = it * GPT + s
                    pe.wait_ge(R.gathered[s], 16 * TPG * it + 16 * TPG)
                    pe.wait_ge(R.S_built, g + 1)
                    pe.wait_ge(R.out_ready, g)
                    pe.wait_ge(R.idx_ready, g)
                    for t in range(TPG):
                        last = pe.matmul(banks[t // 3][:, (t % 3) * (L0 + 1):(t % 3 + 1) * (L0 + 1)],
                                         S0[:, s % 2, t * P:(t + 1) * P], zb[:, s, t, :], start=True, stop=True)
                    last.then_inc(R.joined, 1)

            def edges(R, cols):
                r = R.n - 1
                M = Mflat[:, 0:2 * TPG * cols].rearrange("p (s t c) -> p s t c", s=2, t=TPG)

                def hidden(g, s, turn, first=False):
                    pe.wait_ge(R.ld_rest[s], R.rest * turn + R.rest)
                    for j in range(2):
                        if not first:
                            pe.wait_ge(R.relu, 2 * g + j - 1)
                        pe.matmul(banks[j][:, :], w1_sb[r][:, :], ea[0:H, s, j * 512:(j + 1) * 512],
                                  start=True, stop=True).then_inc(R.hid, 1)

                def weights(g, s, k, first=False):
                    pe.wait_ge(R.relu, 2 * g + k // 2 + 1)
                    if not (first and k < 2):
                        pe.wait_ge(R.prod, 4 * g + k - 1)
                    for j in range(2):
                        t = 2 * k + j
                        last = pe.matmul(wide[k % 2][:, j, 0:WN], hT[0:H + 1, s % 2, t * P:(t + 1) * P],
                                         w2_sb[r][:, :], start=True, stop=True)
                    last.then_inc(R.weights, 1)

                def join(g, s, first=False):
                    pe.wait_ge(R.msgs, g + 1)
                    if not first:
                        pe.wait_ge(R.out_ready, g - 1)
                        pe.wait_ge(R.idx_ready, g - 1)
                    for t in range(TPG):
                        last = pe.matmul(banks[2 + s % 2][:, t * cols:(t + 1) * cols], Sm[:, s % 2, t * P:(t + 1) * P],
                                         M[:, s % 2, t, :], start=True, stop=True)
                    last.then_inc(R.joined, 1)

                def body(it, first, last):
                    for s in range(GPT):
                        g = it * GPT + s
                        f = first and s == 0
                        weights(g, s, 0, f)
                        weights(g, s, 1, f)
                        if not f:
                            join(g - 1, (s - 1) % GPT, first and s <= 2)
                        if not (last and s == GPT - 1):
                            hidden(g + 1, (s + 1) % GPT, it + (s + 1) // GPT)
                        weights(g, s, 2)
                        weights(g, s, 3)

                pe.wait_ge(R.set_up, 1)
                hidden(0, 0, 0, True)
                body(0, True, False)
                with pe.Fori(1, TURNS - 1) as it:
                    body(it, False, False)
                body(TURNS - 1, False, True)
                join(NG - 1, GPT - 1)

            def totals():
                for i in range(2):
                    totals.n += 1
                    pe.wait_ge(part_in, totals.n)
                    pe.matmul(banks[0][:, 0:32], ones[:, :], stat[:, 0, :], start=True, stop=True).then_inc(part_sum, 1)
            totals.n = 0

            edges(RA, COLS_A)
            totals()
            edges(RB, COLS_B)
            totals()

        @block.scalar
        def _(act):
            def root(ap, bias_done, signal_done):
                act.wait_ge(sqrt_in, bias_done)
                act.activation(ap, ap, ACT.Sqrt).then_inc(signal_done, 1)

            root(small[:, 1, :], 1, sqrt_out)
            act.wait_ge(h0_done, 1)
            with act.Fori(0, K0) as k:
                act.wait_ge(zT_done, k)
                act.copy(zh, h_p[:, bass.ds(k * P, P)]).then_inc(zh_done, 1)
                act.wait_ge(zT_done, k + 1)
                act.wait_ge(z_mm, 2 * k)
                act.copy(zTs, banks[0][:, 0:P]).then_inc(zTc_done, 1)
            with act.Fori(0, PIECES) as q:
                act.wait_ge(pc_sq, q + 1)
                act.activation(rootp, rootp, ACT.Sqrt).then_inc(pc_root, 1)

            act.wait_ge(bound_out, 1)
            turns = act.value_load(turns_sb[0:1, 0:1], min_val=1, max_val=TURNS)
            R = R0
            with act.Fori(0, turns) as it:
                for s in range(GPT):
                    g = it * GPT + s
                    act.wait_ge(R.joined, g + 1)
                    act.wait_ge(R.out_free, g + 1)
                    for b in range(3):
                        n = min(3, TPG - 3 * b)
                        last = act.copy(out0[:, s, 3 * b:3 * b + n, :],
                                        banks[b][:, 0:n * (L0 + 1)].rearrange("p (t c) -> p t c", c=L0 + 1)[:, :, 0:L0])
                    last.then_inc(R.out_ready, 1)
            root(small[:, 1, :], 2, sqrt_out)

            def edges(R, cols, row):
                r = R.n - 1
                outv = outflat.rearrange("p (s t c) -> p s t c", s=GPT, t=TPG)

                def relu(g, s, first=False):
                    for j in range(2):
                        act.wait_ge(R.hid, 2 * g + j + 1)
                        if not first and j == 0:
                            act.wait_ge(R.weights, 4 * g - 4)
                        act.activation(hT[0:H, s % 2, j * 512:(j + 1) * 512], banks[j][0:H, :], ACT.Relu,
                                       bias=b1_sb[r][:, :]).then_inc(R.relu, 1)

                def copy_out(g, s):
                    act.wait_ge(R.joined, g + 1)
                    act.wait_ge(R.out_free, g + 1)
                    ps = banks[2 + s % 2][:, 0:TPG * cols].rearrange("p (t c) -> p t c", c=cols)
                    last = act.copy(outv[:, s, :, 0:NS], ps[:, :, 0:NS])
                    if row == ROW_A:
                        last = act.copy(outv[:, s, :, NS:NS + 13], ps[:, :, 20:33])
                    last.then_inc(R.out_ready, 1)

                def body(it, first, last):
                    for s in range(GPT):
                        g = it * GPT + s
                        f = first and s == 0
                        if not f:
                            copy_out(g - 1, (s - 1) % GPT)
                        if not (last and s == GPT - 1):
                            relu(g + 1, (s + 1) % GPT, f)

                act.wait_ge(R.set_up, 1)
                relu(0, 0, True)
                body(0, True, False)
                with act.Fori(1, TURNS - 1) as it:
                    body(it, False, False)
                body(TURNS - 1, False, True)
                copy_out(NG - 1, GPT - 1)

            edges(RA, COLS_A, ROW_A)
            root(stat[:, 3, :], 3, sqrt_out)
            edges(RB, COLS_B, ROW_B)
            root(stat[:, 3, :], 4, sqrt_out)

        @block.vector
        def _(dve):
            tt, ts, red = dve.tensor_tensor, dve.tensor_scalar, dve.tensor_reduce

            def norm_relu(src_, dst_, tmp):
                m, rs = small[:, 0, :], small[:, 1, :]
                link(red(m, k16(src_), AX, ALU.add))
                link(ts(m, m, 1.0 / NS, None, ALU.mult))
                link(tt(k16(dst_), k16(src_), per_node(m, NS), ALU.subtract))
                link(tt(tmp, dst_, dst_, ALU.mult))
                link(red(rs, k16(tmp), AX, ALU.add))
                link(ts(rs, rs, 1.0 / NS, EPS, ALU.mult, ALU.add))
                dve_sqrt(rs)
                link(dve.reciprocal(rs, rs))
                link(tt(k16(dst_), k16(dst_), per_node(rs, NS), ALU.mult))
                return ts(dst_, dst_, 0.0, None, ALU.max)

            dve.memset(zero[:, :], 0.0).then_inc(zero_set, 1)
            dve.memset(ones[:, :], 1.0)
            link(dve.memset(stat[:, :, :], 0.0))
            dve.wait_ge(x_in, 16)
            dve.wait_ge(ld_const, 16 * NCONST)
            link(tt(Mk[:, :].rearrange("p (w b) -> p w b", b=NS), wl[:, :].unsqueeze(2).broadcast_to([P, NT * 8, NS]),
                    cmask[:, :].unsqueeze(1).broadcast_to([P, NT * 8, NS]), ALU.mult))
            norm_relu(xs[:, :], h_p, d_p).then_inc(h0_done, 1)
            half = NT * L0 // 2
            with dve.Fori(0, K0) as k:
                dve.wait_ge(z_out, 16 * k)
                for i in range(2):
                    dve.wait_ge(z_mm, 2 * k + i + 1)
                    tt(zts[:, i * half:(i + 1) * half].rearrange("p (w b) -> p w b", b=NS),
                       banks[1 + i][:, 0:half].rearrange("p (w b) -> p w b", b=NS),
                       bl[:, i * half // NS:(i + 1) * half // NS].unsqueeze(2).broadcast_to([P, half // NS, NS]),
                       ALU.add).then_inc(z_sum, 1)

            dve.memset(vmax[:, :], 1.0).then_inc(psem, 1)
            STEPS = 16
            g3 = lambda v_, c_: v_.rearrange("p (g t) -> p g t", t=c_)
            with dve.Fori(0, PIECES) as q:
                step = [0]

                def pl(ins):
                    step[0] += 1
                    ins.then_inc(psem, 1)
                    dve.wait_ge(psem, STEPS * q + (step[0] + 1))

                dve.wait_ge(pc_in, 80 * q + 80)
                sv = g3(sidep, 4 * TPG)
                s0 = g3(side0p, 2 * TPG)
                pl(tt(shp, vecp, vecp, ALU.mult))
                red(rootp, shp.rearrange("p (e c) -> p e c", c=SH), AX, ALU.add).then_inc(pc_sq, 1)
                pl(ts(t1p, srcp, float(N0 - 1), float(NT), ALU.min, ALU.mult))
                pl(ts(t2p, typp, 0.0, float(NT), ALU.is_equal, ALU.mult))
                pl(tt(t1p, t1p, t2p, ALU.add))
                pl(tt(t1p, t1p, typp, ALU.add))
                pl(ts(zip_i, t1p, -1.0, None, ALU.add))
                pl(dve.tensor_copy(sv[:, :, 24:32], g3(srcp, TPG)))
                pl(dve.tensor_copy(s0[:, :, 0:TPG], g3(dstp, TPG)))
                pl(ts(t1p, dstp, spare0[:, 0:1], None, ALU.subtract))
                pl(ts(t2p, dstp, float(N0), None, ALU.is_lt))
                pl(tt(t1p, t1p, t2p, ALU.mult))
                pl(ts(s0[:, :, TPG:2 * TPG], g3(t1p, TPG), spare0[:, 0:1], None, ALU.add))
                pl(red(t1p[:, 0:PG], g3(t2p, TPG), AX, ALU.max))
                pl(tt(t1p[:, 0:PG], t1p[:, 0:PG], turnp, ALU.mult))
                pl(red(t1p[:, PG:PG + 1], t1p[:, 0:PG], AX, ALU.max))
                dve.wait_ge(pc_root, q + 1)
                pl2 = ts(rootp, rootp, 1e-12, 3.0 ** -0.5, ALU.add, ALU.mult)
                pl(pl2)
                assert step[0] == STEPS, step
                dve.tensor_tensor(vmax[:, 0:1], vmax[:, 0:1], t1p[:, PG:PG + 1], ALU.max).then_inc(qsem, 1)
                dve.reciprocal(rootp, rootp).then_inc(qsem, 1)
                dve.wait_ge(qsem, 2 * q + 2)
                tt(sv[:, :, 0:24].rearrange("p g (t c) -> p g t c", c=SH),
                   vecp.rearrange("p (g t c) -> p g t c", t=TPG, c=SH),
                   g3(rootp, TPG).unsqueeze(3).broadcast_to([P, PG, TPG, SH]), ALU.mult).then_inc(pc_done, 1)
            dve.wait_ge(pc_done, PIECES)
            dve.sem_inc(bound_in, 1)

            dve.wait_ge(pc_out, 48 * PIECES)
            R = R0
            dve.wait_ge(bound_out, 1)
            for s in range(GPT):
                last = dve.tensor_copy(zb[:, s, :, L0], code_sb[:, 0:1].broadcast_to([P, TPG]))
            last.then_inc(R.set_up, 1)
            dve.wait_ge(R.set_up, 1)
            dve.sem_inc(R.x_free, GPT)
            dve.sem_inc(R.inputs_free, GPT)
            turns = dve.value_load(turns_sb[0:1, 0:1], min_val=1, max_val=TURNS)
            with dve.Fori(0, turns) as it:
                for s in range(GPT):
                    g = it * GPT + s
                    dve.wait_ge(R.ld_rest[s], R.rest * it + R.rest)
                    for t in range(TPG):
                        last = ts(S0[:, s % 2, t * P:(t + 1) * P], rowb0[:, s, t * P:(t + 1) * P],
                                  sd0[:, s, t:t + 1], None, ALU.is_equal)
                    last.then_inc(R.S_built, 1)
                    ts(tmp0, sd0[:, s, TPG:2 * TPG], -1.0, spare0[:, 0:1], ALU.mult, ALU.add).then_inc(R.step, 1)
                    dve.wait_ge(R.out_ready, g + 1)
                    dve.wait_ge(R.out_free, g + 1)
                    dve.wait_ge(R.step, 3 * g + 1)
                    for b in range(3):
                        n = min(3, TPG - 3 * b)
                        last = dve.scalar_tensor_tensor(
                            out=tmp0[:, 3 * b:3 * b + n],
                            in0=banks[b][:, 0:n * (L0 + 1)].rearrange("p (t c) -> p t c", c=L0 + 1)[:, :, L0],
                            scalar=code_sb[:, 1:2], in1=tmp0[:, 3 * b:3 * b + n], op0=ALU.is_gt, op1=ALU.mult)
                    last.then_inc(R.step, 1)
                    dve.wait_ge(R.step, 3 * g + 2)
                    tt(ui0[:, s, :], tmp0, sd0[:, s, TPG:2 * TPG], ALU.add).then_inc(R.step, 1)
                    dve.wait_ge(R.step, 3 * g + 3)
                    dve.sem_inc(R.idx_ready, 1)
                    dve.sem_inc(R.x_free, 1)
                    dve.sem_inc(R.inputs_free, 1)

            dve.wait_ge(y_in, 16 * REPL)
            for r in range(REPL):
                link(tt(xs[:, :], xs[:, :], y_st[r], ALU.add))
            norm_relu(xs[:, :], nb[0], nb[1]).then_inc(h1_done, 1)
            dve.wait_ge(h1_out, 16)

            def edges(R, cols, I, J):
                M = Mflat[:, 0:2 * TPG * cols].rearrange("p (s t c) -> p s t c", s=2, t=TPG)
                round_a = cols == COLS_A

                def sh_of(s):
                    return sd[:, s, 0:24].rearrange("p (t c) -> p t c", c=SH).unsqueeze(2).broadcast_to([P, TPG, NV, SH])

                def build_S(g, s, turn, first):
                    dve.wait_ge(R.ld_rest[s], R.rest * turn + R.rest)
                    if not first:
                        dve.wait_ge(R.joined, g - 1)
                    if not round_a:
                        dve.wait_ge(R.gathered[s], 16 * TPG * turn + 16 * TPG)
                        tt(vtmp, xg[:, s, :, 0:NV * SH].rearrange("p t (j c) -> p t j c", c=SH), sh_of(s),
                           ALU.mult).then_inc(R.vec, 1)
                    for t in range(TPG):
                        last = ts(Sm[:, s % 2, t * P:(t + 1) * P], rowb[:, s, t * P:(t + 1) * P],
                                  sd[:, s, 24 + t:25 + t], None, ALU.is_equal)
                    last.then_inc(R.S_built, 1)
                    ts(away[:, s % 2, :], sd[:, s, 24:32], -1.0, spare0[:, 1:2], ALU.mult, ALU.add).then_inc(R.S_built, 1)
                    if not round_a:
                        dve.wait_ge(R.vec, 2 * g + 1)
                        red(xg[:, s, :, 28:32], vtmp, AX, ALU.add).then_inc(R.vec, 1)
                        dve.wait_ge(R.vec, 2 * g + 2)

                def multiply(g, s, k, first):
                    if k == 0 and round_a:
                        dve.wait_ge(R.gathered[s], 16 * TPG * first[1] + 16 * TPG)
                    dve.wait_ge(R.weights, 4 * g + k + 1)
                    if not (first[0] and k < 2):
                        dve.wait_ge(R.red, 4 * g + k - 1)
                    tt(prod[:, k % 2].rearrange("p t (j i) -> p t j i", i=I),
                       wide[k % 2][:, :, 0:WN].rearrange("p t (j i) -> p t j i", i=I),
                       xg[:, s, 2 * k:2 * k + 2, 12:12 + I].unsqueeze(2).broadcast_to([P, 2, J, I]),
                       ALU.mult).then_inc(R.prod, 1)

                def reduce_(g, s, k):
                    dve.wait_ge(R.prod, 4 * g + k + 1)
                    red(M[:, s % 2, 2 * k:2 * k + 2, 0:J], prod[:, k % 2].rearrange("p t (j i) -> p t j i", i=I),
                        AX, ALU.add).then_inc(R.red, 1)

                def targets(g, s):
                    dve.wait_ge(R.out_ready, g + 1)
                    dve.wait_ge(R.out_free, g + 1)
                    ps = banks[2 + s % 2][:, 0:TPG * cols].rearrange("p (t c) -> p t c", c=cols)
                    dve.scalar_tensor_tensor(out=away[:, s % 2, :], in0=ps[:, :, cols - 1], scalar=code_sb[:, 1:2],
                                             in1=away[:, s % 2, :], op0=ALU.is_gt, op1=ALU.mult).then_inc(R.step, 1)
                    dve.wait_ge(R.step, 2 * g + 1)
                    tt(ui[:, s, :], away[:, s % 2, :], sd[:, s, 24:32], ALU.add).then_inc(R.step, 1)
                    dve.wait_ge(R.step, 2 * g + 2)
                    dve.sem_inc(R.idx_ready, 1)
                    dve.sem_inc(R.inputs_free, 1)

                def body(it, first):
                    for s in range(GPT):
                        g = it * GPT + s
                        f = first and s == 0
                        build_S(g, s, it, first and s < 2)
                        for k in range(4):
                            multiply(g, s, k, (f, it))
                            if k:
                                reduce_(g, s, k - 1)
                            if k == 2 and not f:
                                targets(g - 1, (s - 1) % GPT)
                        reduce_(g, s, 3)
                        dve.wait_ge(R.red, 4 * g + 4)
                        dve.sem_inc(R.x_free, 1)
                        if round_a:
                            tt(M[:, s % 2, :, 20:32].rearrange("p t (j c) -> p t j c", c=SH),
                               M[:, s % 2, :, 16:20].unsqueeze(3).broadcast_to([P, TPG, NV, SH]), sh_of(s),
                               ALU.mult).then_inc(R.msgs, 1)
                        else:
                            dve.sem_inc(R.msgs, 1)

                last = dve.memset(hT[:, :, :], 1.0)
                last = dve.memset(Mflat, 1.0)
                last = dve.memset(outflat, 0.0)
                link(last)
                for b in range(2):
                    last = dve.tensor_copy(M[:, b, :, cols - 1], code_sb[:, 0:1].broadcast_to([P, TPG]))
                link(last)
                dve.sem_inc(R.set_up, 1)
                dve.sem_inc(R.x_free, GPT)
                dve.sem_inc(R.inputs_free, GPT)
                body(0, True)
                with dve.Fori(1, TURNS) as it:
                    body(it, False)
                targets(NG - 1, GPT - 1)

            def add_up(n, st, dst_of, row):
                for q in range(TP):
                    dve.wait_ge(t_in[n], 16 * REPL * (q + 1))
                    for r in range(1, REPL):
                        link(tt(st[0], st[0], st[r], ALU.add))
                    dst_of(q, st[0].rearrange("p (k c) -> p k c", c=row))
                    dve.sem_inc(t_used[n], 1)

            edges(RA, COLS_A, NS, NS + NV)

            Tk = T[:, :].rearrange("p (k c) -> p k c", c=TAB)
            pn = [0]

            def piece_a(q, s_):
                ks = slice(q * KP, (q + 1) * KP)
                rc = rcount[:, ks]
                link(ts(rc, s_[:, :, 28], 1.0, None, ALU.max))
                link(dve.reciprocal(rc, rc))
                link(tt(rc, rc, mask[:, ks], ALU.mult))
                rw = lambda w: rc.unsqueeze(2).broadcast_to([P, KP, w])
                link(tt(Tk[:, ks, 0:12], s_[:, :, NS:NS + 12], rw(12), ALU.mult))
                link(tt(Tk[:, ks, 12:28], s_[:, :, 0:NS], rw(NS), ALU.mult))

            def total(src_, w):
                link(red(stat[:, 0, 0:w], src_.rearrange("p k c -> p c k"), AX, ALU.add))
                dve.sem_inc(part_in, 1)
                pn[0] += 1
                dve.wait_ge(part_sum, pn[0])

            def batch_norm(V, w, first_s, gs, bs, gv):
                sq = sqT[:, 0:K * w].rearrange("p (k c) -> p k c", c=w)
                mean, var, scale = stat[:, 1, 0:w], stat[:, 2, 0:w], stat[:, 3, 0:w]
                S_ = slice(first_s, first_s + NS)
                total(V, w)
                link(ts(mean, banks[0][:, 0:w], 1.0 / N, None, ALU.mult))
                if first_s:
                    link(dve.memset(stat[:, 1, 0:first_s], 0.0))
                link(tt(V, V, per_chan(mean, w), ALU.subtract))
                link(tt(sq, V, V, ALU.mult))
                link(tt(sq, sq, per_node(mask[:, :], w), ALU.mult))
                total(sq, w)
                link(ts(var, banks[0][:, 0:w], 1.0 / N, None, ALU.mult))
                if first_s:
                    link(red(stat[:, 4, 0:NV], stat[:, 2, 0:12].rearrange("p (j c) -> p j c", c=SH), AX, ALU.add))
                    link(ts(stat[:, 4, 0:NV], stat[:, 4, 0:NV], 1.0 / SH, None, ALU.mult))
                    link(dve.tensor_copy(stat[:, 2, 0:12].rearrange("p (j c) -> p j c", c=SH),
                                         stat[:, 4, 0:NV].unsqueeze(2).broadcast_to([P, NV, SH])))
                link(ts(scale, var, EPS, None, ALU.add))
                dve_sqrt(scale)
                link(dve.reciprocal(scale, scale))
                link(tt(stat[:, 3, S_], stat[:, 3, S_], gs, ALU.mult))
                if first_s:
                    link(tt(stat[:, 3, 0:12].rearrange("p (j c) -> p j c", c=SH),
                            stat[:, 3, 0:12].rearrange("p (j c) -> p j c", c=SH),
                            gv.unsqueeze(2).broadcast_to([P, NV, SH]), ALU.mult))
                    link(ts(stat[:, 3, 0:12], stat[:, 3, 0:12], 3.0 ** -0.5, None, ALU.mult))
                link(tt(V, V, per_chan(scale, w), ALU.mult))
                link(tt(V[:, :, S_], V[:, :, S_], per_chan(bs, NS), ALU.add))

            add_up(0, stA, piece_a, ROW_A)
            link(ts(T[:, :], T[:, :], NS ** -0.5, None, ALU.mult))
            batch_norm(Tk, TAB, 12, bn[:, 0:NS], bn[:, NS:2 * NS], bn[:, 4 * NS:4 * NS + NV])
            dve.sem_inc(s_done, 1)
            dve.wait_ge(s_out, 16)

            edges(RB, COLS_B, NS + NV, NS)
            Vb = T[:, 0:XW].rearrange("p (k c) -> p k c", c=NS)

            def piece_b(q, s_):
                ks = slice(q * KP, (q + 1) * KP)
                link(tt(Vb[:, ks, :], s_, rcount[:, ks].unsqueeze(2).broadcast_to([P, KP, NS]), ALU.mult))

            add_up(1, stB, piece_b, ROW_B)
            link(ts(T[:, 0:XW], T[:, 0:XW], (NS + NV) ** -0.5, None, ALU.mult))
            batch_norm(Vb, NS, 0, bn[:, 2 * NS:3 * NS], bn[:, 3 * NS:4 * NS], None)
            link(tt(xs[:, :], xs[:, :], T[:, 0:XW], ALU.add))
            dve.sem_inc(fin, 1)


NCONST = 18


def lay_out(i):
    f = np.float32
    a = {k: np.asarray(v) for k, v in i.items()}
    N, E = a["x"].shape[0], a["src"].shape[0]
    K = -(-N // (P * 8)) * 8
    NP = P * K
    step = EPG * GPT * PIECES // 4
    EP = -(-E // step) * step
    NG = EP // EPG
    pad = EP - E

    def fill(v, value):
        return np.concatenate([v, np.full((pad,) + v.shape[1:], value, v.dtype)])

    src, dst, typ = fill(a["src"], N), fill(a["dst"], N - 1), fill(a["edge_type_6"], 1)
    if NP == N:
        raise ValueError("needs a padded node")
    cols = lambda v: np.ascontiguousarray(v.reshape(EP // P, P).T)
    vec = fill(a["edge_attr_3"], 0)
    w_t = a["L0_gnn_W"].transpose(2, 0, 1).reshape(8, NT * 8)

    def second(w, b, vec_major):
        w = np.concatenate([w, b[None]])
        wa = w[:, :NS * NS].reshape(-1, NS, NS)
        if vec_major:
            wb = w[:, NS * NS:].reshape(-1, NV, NS)
            full = np.concatenate([wa, wb], 1)
        else:
            wb = w[:, NS * NS:].reshape(-1, NS, NV)
            full = np.concatenate([wa, wb], 2)
        return np.ascontiguousarray(full.transpose(0, 2, 1).reshape(-1, WN))

    p = np.arange(P)
    arr = {
        "x": np.concatenate([a["x"], np.zeros((NP - N, NS), f)]).reshape(P, K * NS),
        "src_cols": cols(src), "dst_cols": cols(dst), "typ_cols": cols(typ),
        "vec_cols": np.ascontiguousarray(vec.reshape(EP // P, P, 3).transpose(1, 0, 2).reshape(P, -1)),
        "src_row": src, "dst_row": dst,
        "attr": np.ascontiguousarray(fill(a["edge_attr_48"], 0).T),
        "turn_no": np.tile((np.arange(NG) // GPT + 1).astype(f), (P, 1)),
        "ident": np.eye(P, dtype=f),
        "code": np.stack([3.0 ** (64 - p), 2 * 3.0 ** (64 - p)], 1).astype(f),
        "spare": np.stack([NP // 8 + p, NP + p], 1).astype(f),
        "node_mask": (np.arange(NP) < N).astype(f).reshape(P, K),
        "copy_mask": (p[:, None] % NS == np.arange(NS)[None]).astype(f),
        "w_l0": np.repeat(w_t, NS, axis=0),
        "b_l0": a["L0_gnn_Bv"].reshape(-1),
        "w1": np.pad(np.stack([a["L1_gnn_fc0_w1"], a["L1_gnn_fc1_w1"]]), ((0, 0), (0, 0), (0, P - H))),
        "b1": np.stack([a["L1_gnn_fc0_b1"], a["L1_gnn_fc1_b1"]])[:, :, None],
        "w2a": second(a["L1_gnn_fc0_w2"], a["L1_gnn_fc0_b2"], False),
        "w2b": second(a["L1_gnn_fc1_w2"], a["L1_gnn_fc1_b2"], True),
        "gs0": a["L1_gnn_bn0_gs"], "bs0": a["L1_gnn_bn0_bs"], "gv0": a["L1_gnn_bn0_gv"],
        "gs1": a["L1_gnn_bn1_gs"], "bs1": a["L1_gnn_bn1_bs"],
    }
    return {k: np.ascontiguousarray(v) for k, v in arr.items()}, N, NG, K


def kernel(**inputs):
    import concourse.bacc as bacc
    from concourse.bass_utils import run_bass_kernel_spmd

    arrays, N, NG, K = lay_out(inputs)
    nc = bacc.Bacc("TRN2", target_bir_lowering=False, num_devices=1)
    aps = {k: nc.dram_tensor("in_" + k, v.shape, mybir.dt.from_np(v.dtype), kind="ExternalInput").ap()
           for k, v in arrays.items()}
    out = nc.dram_tensor("out_x", (P, K * NS), F32, kind="ExternalOutput").ap()
    build(nc, N, NG, out=out, **aps)
    r = run_bass_kernel_spmd(nc, [{"in_" + k: v for k, v in arrays.items()}], core_ids=[0])
    return r.results[0]["out_x"].reshape(P * K, NS)[:N]
```

```python
from contextlib import ExitStack

import numpy as np
import concourse.bass as bass
from concourse import mybir

F32 = mybir.dt.float32
I32 = mybir.dt.int32
U16 = mybir.dt.uint16
BF16 = mybir.dt.bfloat16
ALU = mybir.AluOpType
ACT = mybir.ActivationFunctionType
AX = mybir.AxisListType.X
RMAX = bass.bass_isa.ReduceOp.max

P = 128
TPG = 8
GPT = 4
EPG = P * TPG
REPL = 4
EPS = 1e-5
NS, NV, SH = 16, 4, 3
H = 48
WN = NS * NS + NS * NV
NT = 5
L0 = 8 * NS
ROW_A = 32
ROW_B = NS
COLS_A = 34
COLS_B = NS + 1
LIVE = (COLS_A - 2, COLS_B - 1)
TAB = NV * SH + NS
PIECES = 8
ZW = 1280


def build(nc, N, NG, x, src_cols, dst_cols, typ_cols, vec_cols, src_row, dst_row, attr, turn_no,
          ident, code, spare, node_mask, copy_mask, w_l0, b_l0, w1, b1, w2a, w2b,
          gs0, bs0, gv0, gs1, bs1, out):
    K = x.shape[1] // NS
    NP = P * K
    N0 = N // 8
    K0 = K // 8
    NP0 = P * K0
    TT = NG * TPG
    TURNS = NG // GPT
    PG = NG // PIECES
    XW = K * NS

    def dram(name, shape, dt=F32):
        return nc.dram_tensor(name, shape, dt, kind="Internal").ap()

    z_tab = dram("z_tab", (NP0 * NT, L0))
    z_idx = dram("z_idx", (P, TT), I32)
    side0 = dram("side0", (P, NG * 2 * TPG))
    side = dram("side", (P, NG * 4 * TPG))
    src16 = dram("src16", (NG * EPG,), U16)
    rel16 = dram("rel16", (NG * EPG,), BF16)
    first_d = dram("first_d", (NG,), I32)
    wide_d = dram("wide_d", (NG,), I32)
    h_tab = dram("h_tab", (NP, NS))
    s_tab = dram("s_tab", (NP, TAB))
    h_parts = dram("h_parts", (NP, 3 * NS), BF16)
    s_parts = dram("s_parts", (NP, 3 * TAB), BF16)
    acc0 = [dram(f"acc0_{r}", (NP0 + P, L0)) for r in range(REPL)]
    accA = [dram(f"accA_{r}", (NP + P, ROW_A)) for r in range(REPL)]
    accB = [dram(f"accB_{r}", (NP + P, ROW_B)) for r in range(REPL)]

    with ExitStack() as ctx:
        def sb(name, shape, dt=F32):
            return ctx.enter_context(nc.sbuf_tensor(name, shape, dt))

        def sem(name):
            return ctx.enter_context(nc.semaphore(name))

        xs = sb("xs", [P, XW])
        T = sb("T", [P, K * TAB])
        rcount = sb("rcount", [P, K])
        mask = sb("mask", [P, K])
        small = sb("small", [P, 4, K])
        ident_sb = sb("ident_sb", [P, P])
        ones = sb("ones", [P, P])
        code_sb = sb("code_sb", [P, 2])
        spare0 = sb("spare0", [P, 3])
        cmask = sb("cmask", [P, NS])
        wl = sb("wl", [P, NT * 8])
        bl = sb("bl", [P, NT * 8])
        Mk = sb("Mk", [P, NT * L0])
        w1_sb = [sb(f"w1_{r}", [P, P]) for r in range(2)]
        b1_sb = [sb(f"b1_{r}", [P, 1]) for r in range(2)]
        w2_sb = [sb(f"w2_{r}", [P, 2 * WN]) for r in range(2)]
        bn = sb("bn", [P, 5 * NS])
        stat = sb("stat", [P, 8, 32])
        vmax = sb("vmax", [P, 2])
        last_turn_sb = sb("last_turn_sb", [P, 1], I32)
        first_sb = sb("first_sb", [1, NG], I32)
        wide_sb = sb("wide_sb", [1, NG + 2 * GPT], I32)
        wide_turn = sb("wide_turn", [1, TURNS + 1], I32)
        zero = sb("zero", [P, ZW])
        ARENA = max(20480, K * TAB * 5 // 2, 4 * XW)
        arena = sb("arena", [P, ARENA])

        def carve(sizes):
            views, at = [], 0
            for n in sizes:
                views.append(arena[:, at:at + n])
                at += n
            assert at <= ARENA, at
            return views

        banks = [ctx.enter_context(nc.psum_tensor(f"bank{i}", [P, 512], F32)) for i in range(4)]
        wide = [ctx.enter_context(nc.psum_tensor(f"wide{i}", [P, 2, 512], F32)) for i in range(2)]

        ld_const = sem("ld_const")
        zeroed = sem("zeroed")
        zero_set = sem("zero_set")
        c = sem("dve_step")
        chain = [0]
        sqrt_in = sem("sqrt_in")
        sqrt_out = sem("sqrt_out")
        nsq = [0]

        block = ctx.enter_context(nc.Block())

        def k16(t):
            return t.rearrange("p (k c) -> p k c", c=NS)

        def per_node(v, w):
            return v.unsqueeze(2).broadcast_to([P, K, w])

        def per_chan(v, w):
            return v.unsqueeze(1).broadcast_to([P, K, w])

        def link(ins):
            chain[0] += 1
            ins.then_inc(c, 1)
            nc.vector.wait_ge(c, chain[0])

        def dve_sqrt(ap):
            nsq[0] += 1
            nc.vector.sem_inc(sqrt_in, 1)
            nc.vector.wait_ge(sqrt_out, nsq[0])

        def wait_past(eng, sem_, count):
            if not isinstance(count, int) or count > 0:
                eng.wait_ge(sem_, count)

        x_in = sem("x_in")
        h0_done = sem("h0_done")
        zT_done, zTc_done, z_mm, z_sum, z_out = (sem(s) for s in ("zT_done", "zTc_done", "z_mm", "z_sum", "z_out"))
        pc_in, pc_done, pc_out = sem("pc_in"), sem("pc_done"), sem("pc_out")
        pc_sq, pc_root = sem("pc_sq"), sem("pc_root")
        psem, qsem = sem("pc_step"), sem("pc_tail")
        bound_in, bound_red, bound_out = sem("bound_in"), sem("bound_red"), sem("bound_out")
        l0_done = sem("l0_done")
        wide_idx, wide_rows, wide_in, wide_max, row_in = (
            sem(s) for s in ("wide_idx", "wide_rows", "wide_in", "wide_max", "row_in"))
        paced, zh_done = sem("paced"), sem("zh_done")
        y_in, y_used = sem("y_in"), sem("y_used")
        h1_done, h1_out = sem("h1_done"), sem("h1_out")
        rA_done, rB_done = sem("rA_done"), sem("rB_done")
        t_in = [sem("tA_in"), sem("tB_in")]
        t_used = [sem("tA_used"), sem("tB_used")]
        part_in, part_sum = sem("part_in"), sem("part_sum")
        s_done, s_out = sem("s_done"), sem("s_out")
        fin, fin_out = sem("fin"), sem("fin_out")

        h_p, d_p, zTs, zh, zts = carve([XW, XW, P, P, NT * L0])
        used = 2 * XW + P + NT * L0
        W8 = PG * TPG
        at = [0]
        srcp, dstp, typp, vecp, shp, rootp, t1p, t2p, sidep, side0p, zip_, turnp, srow, drow, src16p, rel16p, gstat = carve(
            [W8, W8, W8, 3 * W8, 3 * W8, W8, W8, W8, 4 * W8, 2 * W8, W8, PG, EPG, EPG, EPG // 2, EPG // 2, 8])
        srow, drow = srow.bitcast(I32), drow.bitcast(I32)
        src16p, rel16p = src16p.bitcast(U16), rel16p.bitcast(BF16)
        gfirst, gwide = gstat[:, 4:5].bitcast(I32), gstat[:, 5:6].bitcast(I32)
        srcp, dstp, typp, zip_i = srcp.bitcast(I32), dstp.bitcast(I32), typp.bitcast(I32), zip_.bitcast(I32)

        v = carve([GPT * EPG, GPT * TPG * (L0 + 1), GPT * TPG * L0, 2 * EPG, GPT * TPG, GPT * 2 * TPG, GPT * TPG, TPG])
        rowb0 = v[0].bitcast(I32).rearrange("p (s e) -> p s e", s=GPT)
        zb = v[1].rearrange("p (s t c) -> p s t c", s=GPT, t=TPG)
        out0 = v[2].rearrange("p (s t c) -> p s t c", s=GPT, t=TPG)
        S0 = v[3].rearrange("p (s e) -> p s e", s=2)
        zi = v[4].bitcast(I32).rearrange("p (s t) -> p s t", s=GPT)
        sd0 = v[5].rearrange("p (s t) -> p s t", s=GPT)
        ui0 = v[6].bitcast(I32).rearrange("p (s t) -> p s t", s=GPT)
        tmp0 = v[7]

        PT = 3 * TPG
        v = carve([GPT * EPG // 2, GPT * EPG // 2, GPT * EPG // 2, GPT * TPG * 32, 2 * 2 * WN, EPG, EPG, EPG,
                   2 * TPG * COLS_A, 3 * TPG * COLS_A, GPT * TPG * ROW_A, TPG, GPT * 4 * TPG, GPT * TPG, GPT * TPG,
                   GPT * TPG, TPG * NV * SH, GPT * 3 * TAB // 2, EPG])
        srow16 = v[0].bitcast(U16).rearrange("p (s e) -> p s e", s=GPT)
        drow16 = v[1].bitcast(BF16).rearrange("p (s e) -> p s e", s=GPT)
        ea = v[2].rearrange("p (s e) -> p s e", s=GPT)
        xg = v[3].rearrange("p (s t c) -> p s t c", s=GPT, t=TPG)
        prod = v[4].rearrange("p (s t w) -> p s t w", s=2, t=2)
        Sm = v[5].bitcast(BF16).rearrange("p (s e) -> p s e", s=2)
        hT = v[6].rearrange("p (s e) -> p s e", s=2)
        G = v[7].bitcast(BF16).rearrange("p (s e) -> p s e", s=2)
        Mflat = v[8]
        Mparts = v[9].bitcast(BF16)
        outflat = v[10]
        di = v[11].bitcast(I32)
        sd = v[12].rearrange("p (s t) -> p s t", s=GPT)
        ui = v[13].bitcast(I32).rearrange("p (s t) -> p s t", s=GPT)
        away = v[14].rearrange("p (s t) -> p s t", s=GPT)
        home = v[15].rearrange("p (s t) -> p s t", s=GPT)
        vtmp = v[16].rearrange("p (t j c) -> p t j c", j=NV, c=SH)
        window = v[17].bitcast(BF16).rearrange("p (s c) -> p s c", s=GPT)
        dist = v[18]

        y_st = carve([XW] * REPL)
        TP = 4
        KP = K // TP
        stA = carve([KP * ROW_A] * REPL)
        stB = carve([KP * ROW_B] * REPL)
        sqT = carve([K * TAB])[0]
        nb = carve([XW, XW, 3 * XW // 2])
        hparts = nb[2].bitcast(BF16)
        sparts = carve([K * TAB, 3 * K * TAB // 2])[1].bitcast(BF16)

        class EdgeLoop:

            def __init__(r, name, n):
                r.n = n
                r.ld_rest = [sem(f"{name}_rest{s}") for s in range(GPT)]
                r.rest = 16 * (6 if n else 2)
                r.summed = [sem(f"{name}_summed{q}") for q in range(REPL)]
                r.inputs_free = sem(name + "_inputs_free")
                r.x_free = sem(name + "_x_free")
                r.out_free = sem(name + "_out_free")
                r.S_built = sem(name + "_S_built")
                r.joined = sem(name + "_joined")
                r.out_ready = sem(name + "_out_ready")
                r.idx_ready = sem(name + "_idx_ready")
                r.set_up = sem(name + "_set_up")
                r.step = sem(name + "_step")
                if n == 0:
                    r.ld_idx = [sem(f"{name}_idx{s}") for s in range(GPT)]
                    r.gathered = [sem(f"{name}_gathered{s}") for s in range(GPT)]
                    return
                r.G_built = sem(name + "_G_built")
                r.picked = sem(name + "_picked")
                r.x_copied = sem(name + "_x_copied")
                r.x_ready = sem(name + "_x_ready")
                r.cast = sem(name + "_cast")
                r.rest_left = sem(name + "_rest_left")
                r.parted = sem(name + "_parted")
                r.hop = sem(name + "_hop")
                r.rows_free = sem(name + "_rows_free")
                r.hid = sem(name + "_hid")
                r.relu = sem(name + "_relu")
                r.weights = sem(name + "_weights")
                r.prod = sem(name + "_prod")
                r.red = sem(name + "_red")
                r.vec = sem(name + "_vec")
                r.squared = sem(name + "_squared")
                r.msgs = sem(name + "_msgs")

        R0, RA, RB = EdgeLoop("l0", 0), EdgeLoop("a", 1), EdgeLoop("b", 2)

        @block.sync
        def _(sp):
            sp.dma_start(xs[:, :], x).then_inc(x_in, 16)
            n = 0
            for dst_, src_ in ((ident_sb[:, :], ident), (code_sb[:, :], code), (spare0[:, :], spare),
                               (mask[:, :], node_mask), (cmask[:, :], copy_mask), (wl[:, :], w_l0),
                               (bl[:, :], b_l0.partition_broadcast(P)), (w1_sb[0][:, :], w1[0]),
                               (w1_sb[1][:, :], w1[1]), (b1_sb[0][:, :], b1[0]), (b1_sb[1][:, :], b1[1]),
                               (w2_sb[0][:, :], w2a), (w2_sb[1][:, :], w2b),
                               (bn[:, 0:NS], gs0.partition_broadcast(P)), (bn[:, NS:2 * NS], bs0.partition_broadcast(P)),
                               (bn[:, 2 * NS:3 * NS], gs1.partition_broadcast(P)),
                               (bn[:, 3 * NS:4 * NS], bs1.partition_broadcast(P)),
                               (bn[:, 4 * NS:4 * NS + NV], gv0.partition_broadcast(P))):
                sp.dma_start(dst_, src_).then_inc(ld_const, 16)
                n += 1
            assert n == NCONST

            z_rows = z_tab.rearrange("(p k t) c -> p k (t c)", p=P, t=NT)

            def z_store(k):
                sp.wait_ge(z_sum, 2 * k + 2)
                sp.dma_start(z_rows[:, bass.ds(k, 1), :].rearrange("p a c -> p (a c)"), zts).then_inc(z_out, 16)

            z_store(0)
            with sp.Fori(1, K0) as k:
                z_store(k)
            sp.wait_ge(z_out, 16 * K0)

            src_rows = src_row.rearrange("(g e) -> g e", e=EPG)
            dst_rows = dst_row.rearrange("(g e) -> g e", e=EPG)

            def piece(q):
                wait_past(sp, pc_out, 112 * q)
                sp.dma_start(srcp, src_cols[:, bass.ds(q * W8, W8)]).then_inc(pc_in, 16)
                sp.dma_start(dstp, dst_cols[:, bass.ds(q * W8, W8)]).then_inc(pc_in, 16)
                sp.dma_start(typp, typ_cols[:, bass.ds(q * W8, W8)]).then_inc(pc_in, 16)
                sp.dma_start(vecp, vec_cols[:, bass.ds(q * 3 * W8, 3 * W8)]).then_inc(pc_in, 16)
                sp.dma_start(turnp, turn_no[:, bass.ds(q * PG, PG)]).then_inc(pc_in, 16)
                sp.dma_start(srow[0:PG, :], src_rows[bass.ds(q * PG, PG), :]).then_inc(pc_in, 16)
                sp.dma_start(drow[0:PG, :], dst_rows[bass.ds(q * PG, PG), :]).then_inc(pc_in, 16)
                sp.wait_ge(pc_done, q + 1)
                sp.dma_start(side[:, bass.ds(q * 4 * W8, 4 * W8)], sidep).then_inc(pc_out, 16)
                sp.dma_start(side0[:, bass.ds(q * 2 * W8, 2 * W8)], side0p).then_inc(pc_out, 16)
                sp.dma_start(z_idx[:, bass.ds(q * W8, W8)], zip_i).then_inc(pc_out, 16)
                sp.dma_start(src16.rearrange("(g e) -> g e", e=EPG)[bass.ds(q * PG, PG), :], src16p[0:PG, :]).then_inc(pc_out, 16)
                sp.dma_start(rel16.rearrange("(g e) -> g e", e=EPG)[bass.ds(q * PG, PG), :], rel16p[0:PG, :]).then_inc(pc_out, 16)
                sp.dma_start(first_d.unsqueeze(1)[bass.ds(q * PG, PG), :], gfirst[0:PG, :]).then_inc(pc_out, 16)
                sp.dma_start(wide_d.unsqueeze(1)[bass.ds(q * PG, PG), :], gwide[0:PG, :]).then_inc(pc_out, 16)

            piece(0)
            with sp.Fori(1, PIECES) as q:
                piece(q)
            sp.wait_ge(pc_out, 112 * PIECES)
            sp.dma_start(first_sb[:, :], first_d.unsqueeze(0)).then_inc(row_in, 16)
            sp.dma_start(wide_sb[:, 0:NG], wide_d.unsqueeze(0)).then_inc(wide_in, 16)

            sp.wait_ge(bound_out, 1)
            turns = sp.value_load(last_turn_sb[0:1, 0:1], min_val=2, max_val=TURNS - 1) + 1

            def inputs0(it):
                for s in range(GPT):
                    g = it * GPT + s
                    sp.wait_ge(R0.inputs_free, g + 1)
                    sp.dma_start(zi[:, s, :], z_idx[:, bass.ds(g * TPG, TPG)]).then_inc(R0.ld_idx[s], 16)
                    sp.dma_start(sd0[:, s, :], side0[:, bass.ds(g * 2 * TPG, 2 * TPG)]).then_inc(R0.ld_rest[s], 16)
                    sp.dma_start(rowb0[:, s, :], dst_row[bass.ds(g * EPG, EPG)].partition_broadcast(P)).then_inc(R0.ld_rest[s], 16)

            with sp.Fori(0, turns) as it:
                inputs0(it)

            sp.wait_ge(l0_done, 1)
            for r in range(REPL):
                sp.dma_start(y_st[r], acc0[r][0:NP0, :].rearrange("(p k) c -> p (k c)", p=P)).then_inc(y_in, 16)
            sp.wait_ge(h1_done, 1)
            sp.dma_start(h_tab.rearrange("(p k) c -> p (k c)", p=P), nb[0]).then_inc(h1_out, 16)
            sp.wait_ge(h1_done, 2)
            sp.dma_start(h_parts.rearrange("(p k) c -> p (k c)", p=P), hparts).then_inc(h1_out, 16)
            sp.wait_ge(h1_out, 32)

            sp.wait_ge(row_in, 16)

            HE = EPG // 2

            def feed(R, tab, width):
                with sp.Fori(0, TURNS) as it:
                    for s in range(GPT):
                        g = it * GPT + s
                        first = sp.value_load(first_sb[0:1, bass.ds(g, 1)], min_val=0, max_val=NP - P)
                        sp.wait_ge(R.inputs_free, g + 1)
                        sp.wait_ge(R.rows_free, g + 1)
                        for j in range(2):
                            sp.dma_start(ea[64 * j:64 * j + H, s, :], attr[:, bass.ds(g * EPG + j * HE, HE)]).then_inc(R.ld_rest[s], 16)
                        sp.dma_start(srow16[:, s, :], src16[bass.ds(g * EPG, EPG)].partition_broadcast(P)).then_inc(R.ld_rest[s], 16)
                        sp.dma_start(drow16[:, s, :], rel16[bass.ds(g * EPG, EPG)].partition_broadcast(P)).then_inc(R.ld_rest[s], 16)
                        sp.dma_start(sd[:, s, :], side[:, bass.ds(g * 4 * TPG, 4 * TPG)]).then_inc(R.ld_rest[s], 16)
                        sp.dma_start(window[:, s, 0:3 * width], tab[bass.ds(first, P), :]).then_inc(R.ld_rest[s], 16)

            def tables(R, acc, st, row, n):
                for q in range(TP):
                    if q:
                        sp.wait_ge(t_used[n], q)
                    for r in range(REPL):
                        sp.dma_start(st[r], acc[r][0:NP, :].rearrange("(p k) c -> p (k c)", p=P)
                                     [:, q * KP * row:(q + 1) * KP * row]).then_inc(t_in[n], 16)

            feed(RA, h_parts, NS)
            sp.wait_ge(rA_done, 1)
            tables(RA, accA, stA, ROW_A, 0)
            sp.wait_ge(s_done, 1)
            sp.dma_start(s_tab.rearrange("(p k) c -> p (k c)", p=P), T[:, :]).then_inc(s_out, 16)
            sp.wait_ge(s_done, 2)
            sp.dma_start(s_parts.rearrange("(p k) c -> p (k c)", p=P), sparts).then_inc(s_out, 16)
            sp.wait_ge(s_out, 32)
            feed(RB, s_parts, TAB)
            sp.wait_ge(rB_done, 1)
            tables(RB, accB, stB, ROW_B, 1)
            sp.wait_ge(fin, 1)
            sp.dma_start(out, xs[:, :]).then_inc(fin_out, 16)
            sp.wait_ge(fin_out, 16)

        @block.gpsimd
        def _(pool):
            last_row = {rows: pool.to_reg(rows - 1) for rows in sorted({NP0 * NT, NP, NP0 + P, NP + P})}

            def gather(dst_, tab, idx, signal):
                pool.indirect_dma_start(out=dst_, out_offset=None, in_=tab,
                                        in_offset=bass.IndirectOffsetOnAxis(ap=idx, axis=0),
                                        bounds_check=last_row[tab.shape[0]], oob_is_err=True).then_inc(signal, 16)

            def add_rows(tab, src_, idx, signal):
                pool.indirect_dma_start(out=tab, out_offset=bass.IndirectOffsetOnAxis(ap=idx, axis=0),
                                        in_=src_, in_offset=None, bounds_check=last_row[tab.shape[0]],
                                        oob_is_err=True, compute_op=ALU.add).then_inc(signal, 16)

            pool.wait_ge(zero_set, 1)
            n = 0
            for acc in acc0 + accA + accB:
                flat = acc.rearrange("(p k) c -> p (k c)", p=P)
                w = flat.shape[1]
                for a in range(0, w, ZW):
                    b = min(w, a + ZW)
                    pool.dma_start(flat[:, a:b], zero[:, 0:b - a]).then_inc(zeroed, 16)
                    n += 1
            pool.wait_ge(zeroed, 16 * n)

            pool.wait_ge(bound_in, 1)
            pool.partition_all_reduce(vmax[:, 1:2], vmax[:, 0:1], P, RMAX).then_inc(bound_red, 1)
            pool.wait_ge(bound_red, 1)
            pool.tensor_copy(last_turn_sb[:, :], vmax[:, 1:2]).then_inc(bound_out, 1)
            pool.wait_ge(bound_out, 1)
            last_turn = pool.value_load(last_turn_sb[0:1, 0:1], min_val=2, max_val=TURNS - 1)

            R = R0
            pool.wait_ge(z_out, 16 * K0)

            def scatter(R, g, s, acc, rows, idx, between):
                pool.wait_ge(R.out_ready, g + 1)
                pool.wait_ge(R.idx_ready, g + 1)
                for t in range(TPG):
                    wait_past(pool, R.summed[t % REPL], 16 * (TPG // REPL) * g + 16 * (t // REPL))
                    pool.sem_inc(paced, 1)
                    add_rows(acc[t % REPL], rows[:, s, t, :], idx[:, s, t:t + 1], R.summed[t % REPL])
                    between(t)
                pool.sem_inc(R.out_free, 1)

            def fetch0_waits(g, s, turn):
                pool.wait_ge(R.ld_idx[s], 16 * turn + 16)
                pool.wait_ge(R.x_free, g + 1)
                pool.sem_inc(paced, 1)

            def fetch0(s, t):
                gather(zb[:, s, t, 0:L0], z_tab, zi[:, s, t:t + 1], R.gathered[s])

            def body0(it, last):
                for s in range(GPT):
                    g = it * GPT + s
                    ahead = (s + 2) % GPT
                    more = not (last and s + 2 >= GPT)
                    if more:
                        fetch0_waits(g + 2, ahead, it + (s + 2) // GPT)
                    scatter(R, g, s, acc0, out0, ui0, lambda t: fetch0(ahead, t) if more else None)

            pool.sem_inc(R.out_free, GPT - 1)
            for g in range(2):
                fetch0_waits(g, g, 0)
                for t in range(TPG):
                    fetch0(g, t)
            body0(0, False)
            with pool.Fori(1, last_turn) as it:
                body0(it, False)
            body0(last_turn, True)
            for r in range(REPL):
                pool.wait_ge(R.summed[r], 16 * (TPG // REPL) * GPT * (last_turn + 1))
            pool.sem_inc(l0_done, 1)

            def edges(R, tab, width, acc, row, xcols):
                rows = outflat.rearrange("p (s t c) -> p s t c", s=GPT, t=TPG)[:, :, :, 0:row]

                def hand_over(g, s, wide):
                    pool.wait_ge(R.x_copied, g + 1)
                    pool.sem_inc(paced, 1)
                    with pool.If(wide > 0):
                        pool.reg_add(fetched, fetched, 1)
                        n = pool.snap(fetched, min_val=1, max_val=2 * NG)
                        pool.dma_start(di, dst_cols[:, bass.ds(g * TPG, TPG)]).then_inc(wide_idx, 16)
                        pool.wait_ge(wide_idx, 16 * n)
                        pool.sem_inc(paced, 1)
                        for t in range(TPG):
                            gather(xg[:, s, t, xcols:xcols + width], tab, di[:, t:t + 1], wide_rows)
                        pool.wait_ge(wide_rows, 16 * TPG * n)
                        pool.sem_inc(paced, 1)
                    pool.sem_inc(R.x_ready, 1)

                def body(it, last):
                    wide = pool.value_load(wide_turn[0:1, bass.ds(it + 1, 1)], min_val=0, max_val=1)
                    for s in range(GPT):
                        g = it * GPT + s
                        if not (last and s + 3 >= GPT):
                            hand_over(g + 3, (s + 3) % GPT, wide)
                        scatter(R, g, s, acc, rows, ui, lambda t: None)

                pool.sem_inc(R.out_free, GPT - 1)
                wide = pool.value_load(wide_turn[0:1, 0:1], min_val=0, max_val=1)
                for g in range(3):
                    hand_over(g, g, wide)
                body(0, False)
                with pool.Fori(1, TURNS - 1) as it:
                    body(it, False)
                body(TURNS - 1, True)
                for r in range(REPL):
                    pool.wait_ge(R.summed[r], 16 * (TPG // REPL) * NG)

            pool.wait_ge(wide_max, 1)
            fetched = pool.alloc_register("fetched")
            pool.reg_mov(fetched, 0)
            pool.wait_ge(h1_out, 32)
            edges(RA, h_tab, NS, accA, ROW_A, 12)
            pool.sem_inc(rA_done, 1)
            pool.wait_ge(s_out, 32)
            edges(RB, s_tab, TAB, accB, ROW_B, 0)
            pool.sem_inc(rB_done, 1)

        @block.tensor
        def _(pe):
            pe.wait_ge(h0_done, 1)
            pe.wait_ge(ld_const, 16 * NCONST)

            def z_tile(k):
                wait_past(pe, zTc_done, k)
                pe.wait_ge(zh_done, k + 1)
                pe.transpose(banks[0][:, 0:P], zh, ident_sb[:, :]).then_inc(zT_done, 1)
                pe.wait_ge(zTc_done, k + 1)
                wait_past(pe, z_sum, 2 * k)
                pe.matmul(banks[1][:, 0:NT * L0 // 2], zTs, Mk[:, 0:NT * L0 // 2], start=True, stop=True).then_inc(z_mm, 1)
                pe.matmul(banks[2][:, 0:NT * L0 // 2], zTs, Mk[:, NT * L0 // 2:], start=True, stop=True).then_inc(z_mm, 1)

            z_tile(0)
            with pe.Fori(1, K0) as k:
                z_tile(k)

            pe.wait_ge(bound_out, 1)
            turns = pe.value_load(last_turn_sb[0:1, 0:1], min_val=2, max_val=TURNS - 1) + 1
            R = R0

            def join0(it):
                for s in range(GPT):
                    g = it * GPT + s
                    pe.wait_ge(R.gathered[s], 16 * TPG * it + 16 * TPG)
                    pe.wait_ge(R.S_built, g + 1)
                    wait_past(pe, R.idx_ready, g)
                    for t in range(TPG):
                        last = pe.matmul(banks[t // 3][:, (t % 3) * (L0 + 1):(t % 3 + 1) * (L0 + 1)],
                                         S0[:, s % 2, t * P:(t + 1) * P], zb[:, s, t, :], start=True, stop=True)
                    last.then_inc(R.joined, 1)

            join0(0)
            with pe.Fori(1, turns) as it:
                join0(it)

            def edges(R, cols, width):
                r = R.n - 1
                live = LIVE[r]
                Mp = Mparts[:, 0:3 * TPG * cols].rearrange("p (q t c) -> p q t c", q=3, t=TPG)

                def hidden(g, s, turn):
                    pe.wait_ge(R.ld_rest[s], R.rest * turn + R.rest)
                    wait_past(pe, R.relu, g)
                    pe.matmul(banks[0][:, :], w1_sb[r][:, :], ea[:, s, :],
                              start=True, stop=True).then_inc(R.hid, 1)

                def pick(g, s):
                    pe.wait_ge(R.G_built, g + 1)
                    wait_past(pe, R.x_copied, g)
                    for t in range(TPG):
                        for q in range(3):
                            last = pe.matmul(banks[1][:, t * width:(t + 1) * width], G[:, s % 2, t * P:(t + 1) * P],
                                             window[:, s, q * width:(q + 1) * width], start=(q == 0), stop=(q == 2))
                    last.then_inc(R.picked, 1)

                def weights(g, s, k, first=False):
                    pe.wait_ge(R.relu, g + 1)
                    if not (first and k < 2):
                        pe.wait_ge(R.prod, 4 * g + k - 1)
                    for j in range(2):
                        last = pe.matmul(wide[k % 2][:, j, 0:WN], hT[:, s % 2, k * P:(k + 1) * P],
                                         w2_sb[r][:, j * WN:(j + 1) * WN], start=True, stop=True)
                    last.then_inc(R.weights, 1)

                def join(g, s):
                    pe.wait_ge(R.parted, g + 1)
                    pe.wait_ge(R.S_built, g + 1)
                    wait_past(pe, R.idx_ready, g - 1)
                    for t in range(TPG):
                        for q in range(3):
                            w = cols if q == 0 else live
                            last = pe.matmul(banks[2 + s % 2][:, t * cols:t * cols + w], Sm[:, s % 2, t * P:(t + 1) * P],
                                             Mp[:, q, t, 0:w], start=(q == 0), stop=(q == 2))
                    last.then_inc(R.joined, 1)

                def body(it, first, last):
                    for s in range(GPT):
                        g = it * GPT + s
                        f = first and s == 0
                        weights(g, s, 0, f)
                        weights(g, s, 1, f)
                        if not (last and s == GPT - 1):
                            hidden(g + 1, (s + 1) % GPT, it + (s + 1) // GPT)
                        weights(g, s, 2)
                        if not (last and s + 2 >= GPT):
                            pick(g + 2, (s + 2) % GPT)
                        weights(g, s, 3)
                        if not f:
                            join(g - 1, (s - 1) % GPT)

                pe.wait_ge(R.set_up, 1)
                pick(0, 0)
                hidden(0, 0, 0)
                pick(1, 1)
                body(0, True, False)
                with pe.Fori(1, TURNS - 1) as it:
                    body(it, False, False)
                body(TURNS - 1, False, True)
                join(NG - 1, GPT - 1)

            def totals():
                for i in range(2):
                    totals.n += 1
                    pe.wait_ge(part_in, totals.n)
                    pe.matmul(banks[0][:, 0:32], ones[:, :], stat[:, 0, :], start=True, stop=True).then_inc(part_sum, 1)
            totals.n = 0

            edges(RA, COLS_A, NS)
            totals()
            edges(RB, COLS_B, TAB)
            totals()

        @block.scalar
        def _(act):
            def root(ap, bias_done, signal_done):
                act.wait_ge(sqrt_in, bias_done)
                act.activation(ap, ap, ACT.Sqrt).then_inc(signal_done, 1)

            root(small[:, 1, :], 1, sqrt_out)
            act.wait_ge(h0_done, 1)

            def z_copies(k):
                wait_past(act, zT_done, k)
                act.copy(zh, h_p[:, bass.ds(k * P, P)]).then_inc(zh_done, 1)
                act.wait_ge(zT_done, k + 1)
                wait_past(act, z_mm, 2 * k)
                act.copy(zTs, banks[0][:, 0:P]).then_inc(zTc_done, 1)

            z_copies(0)
            with act.Fori(1, K0) as k:
                z_copies(k)
            with act.Fori(0, PIECES) as q:
                act.wait_ge(pc_sq, q + 1)
                act.activation(rootp, rootp, ACT.Sqrt).then_inc(pc_root, 1)

            act.wait_ge(bound_out, 1)
            turns = act.value_load(last_turn_sb[0:1, 0:1], min_val=2, max_val=TURNS - 1) + 1
            R = R0
            with act.Fori(0, turns) as it:
                for s in range(GPT):
                    g = it * GPT + s
                    act.wait_ge(R.joined, g + 1)
                    act.wait_ge(R.out_free, g + 1)
                    for b in range(3):
                        n = min(3, TPG - 3 * b)
                        last = act.copy(out0[:, s, 3 * b:3 * b + n, :],
                                        banks[b][:, 0:n * (L0 + 1)].rearrange("p (t c) -> p t c", c=L0 + 1)[:, :, 0:L0])
                    last.then_inc(R.out_ready, 1)
            root(small[:, 1, :], 2, sqrt_out)

            def edges(R, cols, row, width, xcols):
                r = R.n - 1
                live = LIVE[r]
                outv = outflat.rearrange("p (s t c) -> p s t c", s=GPT, t=TPG)

                Mp = Mparts[:, 0:3 * TPG * cols].rearrange("p (q t c) -> p q t c", q=3, t=TPG)
                M = Mflat[:, 0:2 * TPG * cols].rearrange("p (s t c) -> p s t c", s=2, t=TPG)

                def relu(g, s, first=False):
                    act.wait_ge(R.hid, g + 1)
                    if not first:
                        act.wait_ge(R.weights, 4 * g - 4)
                    act.activation(hT[:, s % 2, :], banks[0][:, :], ACT.Relu, bias=b1_sb[r][:, :]).then_inc(R.relu, 1)

                def part(g, s, q):
                    if q == 0:
                        act.wait_ge(R.msgs, g + 1)
                        wait_past(act, R.joined, g)
                    else:
                        act.wait_ge(R.rest_left, g + 1)
                    w = cols if q == 0 else live
                    act.copy(Mp[:, q, :, 0:w], M[:, s % 2, :, 0:w]).then_inc(R.cast, 1)

                def distances(g, s, turn, t0):
                    act.wait_ge(R.ld_rest[s], R.rest * turn + R.rest)
                    wait_past(act, R.S_built, g)
                    for t in range(t0, t0 + 4):
                        last = act.activation(dist[:, t * P:(t + 1) * P], srow16[:, s, t * P:(t + 1) * P], ACT.Square,
                                              scale=-1.0, bias=sd[:, s, 24 + t:25 + t])
                    last.then_inc(R.squared, 1)

                def build_S(g, s):
                    act.wait_ge(R.squared, 2 * g + 2)
                    act.sem_inc(R.rows_free, 1)
                    wait_past(act, R.joined, g - 1)
                    act.activation(Sm[:, s % 2, :], dist, ACT.Relu, scale=-2.0, bias=ones[:, 0:1]).then_inc(R.S_built, 1)

                def copy_rows(g, s):
                    act.wait_ge(R.picked, g + 1)
                    act.wait_ge(R.x_free, g + 1)
                    act.copy(xg[:, s, :, xcols:xcols + width],
                             banks[1][:, 0:TPG * width].rearrange("p (t c) -> p t c", c=width)).then_inc(R.x_copied, 1)

                def copy_out(g, s):
                    act.wait_ge(R.joined, g + 1)
                    act.wait_ge(R.out_free, g + 1)
                    ps = banks[2 + s % 2][:, 0:TPG * cols].rearrange("p (t c) -> p t c", c=cols)
                    last = act.copy(outv[:, s, :, 0:NS], ps[:, :, 0:NS])
                    if row == ROW_A:
                        last = act.copy(outv[:, s, :, NS:NS + 13], ps[:, :, 20:33])
                    last.then_inc(R.out_ready, 1)

                def body(it, first, last):
                    for s in range(GPT):
                        g = it * GPT + s
                        f = first and s == 0
                        if not f:
                            part(g - 1, (s - 1) % GPT, 0)
                        if not (first and s < 2):
                            copy_out(g - 2, (s - 2) % GPT)
                        distances(g, s, it, 0)
                        if not f:
                            part(g - 1, (s - 1) % GPT, 1)
                        if not (last and s == GPT - 1):
                            relu(g + 1, (s + 1) % GPT, f)
                        distances(g, s, it, 4)
                        if not (last and s + 2 >= GPT):
                            copy_rows(g + 2, (s + 2) % GPT)
                        build_S(g, s)

                act.sem_inc(R.rows_free, GPT)
                act.wait_ge(R.set_up, 1)
                copy_rows(0, 0)
                relu(0, 0, True)
                copy_rows(1, 1)
                body(0, True, False)
                with act.Fori(1, TURNS - 1) as it:
                    body(it, False, False)
                body(TURNS - 1, False, True)
                part(NG - 1, GPT - 1, 0)
                copy_out(NG - 2, GPT - 2)
                part(NG - 1, GPT - 1, 1)
                copy_out(NG - 1, GPT - 1)

            edges(RA, COLS_A, ROW_A, NS, 12)
            root(stat[:, 3, :], 3, sqrt_out)
            edges(RB, COLS_B, ROW_B, TAB, 0)
            root(stat[:, 3, :], 4, sqrt_out)

        @block.vector
        def _(dve):
            tt, ts, red = dve.tensor_tensor, dve.tensor_scalar, dve.tensor_reduce

            def norm_relu(src_, dst_, tmp):
                m, rs = small[:, 0, :], small[:, 1, :]
                link(red(m, k16(src_), AX, ALU.add))
                link(ts(m, m, 1.0 / NS, None, ALU.mult))
                link(tt(k16(dst_), k16(src_), per_node(m, NS), ALU.subtract))
                link(tt(tmp, dst_, dst_, ALU.mult))
                link(red(rs, k16(tmp), AX, ALU.add))
                link(ts(rs, rs, 1.0 / NS, EPS, ALU.mult, ALU.add))
                dve_sqrt(rs)
                link(dve.reciprocal(rs, rs))
                link(tt(k16(dst_), k16(dst_), per_node(rs, NS), ALU.mult))
                return ts(dst_, dst_, 0.0, None, ALU.max)

            def split(src_, tmp, parts, w):
                p0, p1, p2 = (parts[:, :, q * w:(q + 1) * w] for q in range(3))
                link(dve.tensor_copy(p0, src_))
                link(tt(tmp, src_, p0, ALU.subtract))
                link(dve.tensor_copy(p1, tmp))
                link(tt(p2, tmp, p1, ALU.subtract))

            dve.memset(zero[:, :], 0.0).then_inc(zero_set, 1)
            dve.memset(ones[:, :], 1.0)
            link(dve.memset(stat[:, :, :], 0.0))
            dve.wait_ge(x_in, 16)
            dve.wait_ge(ld_const, 16 * NCONST)
            link(tt(Mk[:, :].rearrange("p (w b) -> p w b", b=NS), wl[:, :].unsqueeze(2).broadcast_to([P, NT * 8, NS]),
                    cmask[:, :].unsqueeze(1).broadcast_to([P, NT * 8, NS]), ALU.mult))
            norm_relu(xs[:, :], h_p, d_p).then_inc(h0_done, 1)
            half = NT * L0 // 2

            def z_finish(k):
                wait_past(dve, z_out, 16 * k)
                for i in range(2):
                    dve.wait_ge(z_mm, 2 * k + i + 1)
                    tt(zts[:, i * half:(i + 1) * half].rearrange("p (w b) -> p w b", b=NS),
                       banks[1 + i][:, 0:half].rearrange("p (w b) -> p w b", b=NS),
                       bl[:, i * half // NS:(i + 1) * half // NS].unsqueeze(2).broadcast_to([P, half // NS, NS]),
                       ALU.add).then_inc(z_sum, 1)

            z_finish(0)
            with dve.Fori(1, K0) as k:
                z_finish(k)

            dve.memset(vmax[:, :], 2.0).then_inc(psem, 1)
            STEPS = 23
            g3 = lambda v_, c_: v_.rearrange("p (g t) -> p g t", t=c_)
            with dve.Fori(0, PIECES) as q:
                step = [0]

                def pl(ins):
                    step[0] += 1
                    ins.then_inc(psem, 1)
                    dve.wait_ge(psem, STEPS * q + (step[0] + 1))

                dve.wait_ge(pc_in, 112 * q + 112)
                sv = g3(sidep, 4 * TPG)
                s0 = g3(side0p, 2 * TPG)
                pl(tt(shp, vecp, vecp, ALU.mult))
                red(rootp, shp.rearrange("p (e c) -> p e c", c=SH), AX, ALU.add).then_inc(pc_sq, 1)
                pl(ts(t1p, srcp, float(N0 - 1), float(NT), ALU.min, ALU.mult))
                pl(ts(t2p, typp, 0.0, float(NT), ALU.is_equal, ALU.mult))
                pl(tt(t1p, t1p, t2p, ALU.add))
                pl(tt(t1p, t1p, typp, ALU.add))
                pl(ts(zip_i, t1p, -1.0, None, ALU.add))
                pl(dve.tensor_copy(sv[:, :, 24:32], g3(srcp, TPG)))
                pl(dve.tensor_copy(s0[:, :, 0:TPG], g3(dstp, TPG)))
                pl(ts(t1p, dstp, spare0[:, 0:1], None, ALU.subtract))
                pl(ts(t2p, dstp, float(N0), None, ALU.is_lt))
                pl(tt(t1p, t1p, t2p, ALU.mult))
                pl(ts(s0[:, :, TPG:2 * TPG], g3(t1p, TPG), spare0[:, 0:1], None, ALU.add))
                pl(red(t1p[:, 0:PG], g3(t2p, TPG), AX, ALU.max))
                pl(tt(t1p[:, 0:PG], t1p[:, 0:PG], turnp, ALU.mult))
                pl(red(t1p[:, PG:PG + 1], t1p[:, 0:PG], AX, ALU.max))
                lo, hi = gstat[0:PG, 0:1], gstat[0:PG, 1:2]
                pl(red(lo, drow[0:PG, :], AX, ALU.min))
                pl(red(hi, drow[0:PG, :], AX, ALU.max))
                pl(ts(lo, lo, float(NP - P), None, ALU.min))
                pl(dve.tensor_copy(gfirst[0:PG, :], lo))
                pl(ts(gwide[0:PG, :], hi, lo, float(P), ALU.subtract, ALU.is_ge))
                pl(ts(rel16p[0:PG, :], drow[0:PG, :], lo, 255.0, ALU.subtract, ALU.min))
                pl(dve.tensor_copy(src16p[0:PG, :], srow[0:PG, :]))
                dve.wait_ge(pc_root, q + 1)
                pl2 = ts(rootp, rootp, 1e-12, 3.0 ** -0.5, ALU.add, ALU.mult)
                pl(pl2)
                assert step[0] == STEPS, step
                dve.tensor_tensor(vmax[:, 0:1], vmax[:, 0:1], t1p[:, PG:PG + 1], ALU.max).then_inc(qsem, 1)
                dve.reciprocal(rootp, rootp).then_inc(qsem, 1)
                dve.wait_ge(qsem, 2 * q + 2)
                tt(sv[:, :, 0:24].rearrange("p g (t c) -> p g t c", c=SH),
                   vecp.rearrange("p (g t c) -> p g t c", t=TPG, c=SH),
                   g3(rootp, TPG).unsqueeze(3).broadcast_to([P, PG, TPG, SH]), ALU.mult).then_inc(pc_done, 1)
            dve.wait_ge(pc_done, PIECES)
            dve.sem_inc(bound_in, 1)

            link(dve.memset(wide_sb[:, NG:NG + 2 * GPT], 0))
            dve.wait_ge(wide_in, 16)
            link(red(wide_turn[:, 0:1], wide_sb[:, 0:3], AX, ALU.max))
            red(wide_turn[:, 1:1 + TURNS], wide_sb[:, 3:3 + NG].rearrange("p (t s) -> p t s", s=GPT),
                AX, ALU.max).then_inc(wide_max, 1)

            dve.wait_ge(pc_out, 112 * PIECES)
            R = R0
            dve.wait_ge(bound_out, 1)
            for s in range(GPT):
                last = dve.tensor_copy(zb[:, s, :, L0], code_sb[:, 0:1].broadcast_to([P, TPG]))
            last.then_inc(R.set_up, 1)
            dve.wait_ge(R.set_up, 1)
            dve.sem_inc(R.x_free, GPT)
            dve.sem_inc(R.inputs_free, GPT)
            turns = dve.value_load(last_turn_sb[0:1, 0:1], min_val=2, max_val=TURNS - 1) + 1
            with dve.Fori(0, turns) as it:
                for s in range(GPT):
                    g = it * GPT + s
                    dve.wait_ge(R.ld_rest[s], R.rest * it + R.rest)
                    for t in range(TPG):
                        last = ts(S0[:, s % 2, t * P:(t + 1) * P], rowb0[:, s, t * P:(t + 1) * P],
                                  sd0[:, s, t:t + 1], None, ALU.is_equal)
                    last.then_inc(R.S_built, 1)
                    ts(tmp0, sd0[:, s, TPG:2 * TPG], -1.0, spare0[:, 0:1], ALU.mult, ALU.add).then_inc(R.step, 1)
                    dve.wait_ge(R.out_ready, g + 1)
                    dve.wait_ge(R.out_free, g + 1)
                    dve.wait_ge(R.step, 3 * g + 1)
                    for b in range(3):
                        n = min(3, TPG - 3 * b)
                        last = dve.scalar_tensor_tensor(
                            out=tmp0[:, 3 * b:3 * b + n],
                            in0=banks[b][:, 0:n * (L0 + 1)].rearrange("p (t c) -> p t c", c=L0 + 1)[:, :, L0],
                            scalar=code_sb[:, 1:2], in1=tmp0[:, 3 * b:3 * b + n], op0=ALU.is_gt, op1=ALU.mult)
                    last.then_inc(R.step, 1)
                    dve.wait_ge(R.step, 3 * g + 2)
                    tt(ui0[:, s, :], tmp0, sd0[:, s, TPG:2 * TPG], ALU.add).then_inc(R.step, 1)
                    dve.wait_ge(R.step, 3 * g + 3)
                    dve.sem_inc(R.idx_ready, 1)
                    dve.sem_inc(R.x_free, 1)
                    dve.sem_inc(R.inputs_free, 1)

            dve.wait_ge(y_in, 16 * REPL)
            for r in range(REPL):
                link(tt(xs[:, :], xs[:, :], y_st[r], ALU.add))
            link(norm_relu(xs[:, :], nb[0], nb[1]))
            dve.sem_inc(h1_done, 1)
            split(k16(nb[0]), k16(nb[1]), hparts.rearrange("p (k c) -> p k c", c=3 * NS), NS)
            dve.sem_inc(h1_done, 1)
            dve.wait_ge(h1_out, 32)

            def edges(R, cols, I, J):
                M = Mflat[:, 0:2 * TPG * cols].rearrange("p (s t c) -> p s t c", s=2, t=TPG)
                round_a = cols == COLS_A
                live = LIVE[R.n - 1]

                def sh_of(s):
                    return sd[:, s, 0:24].rearrange("p (t c) -> p t c", c=SH).unsqueeze(2).broadcast_to([P, TPG, NV, SH])

                def build_G(g, s, turn):
                    dve.wait_ge(R.ld_rest[s], R.rest * turn + R.rest)
                    wait_past(dve, R.picked, g - 1)
                    ts(G[:, s % 2, :], drow16[:, s, :], spare0[:, 2:3], None, ALU.is_equal).then_inc(R.G_built, 1)

                Mp = Mparts[:, 0:3 * TPG * cols].rearrange("p (q t c) -> p q t c", q=3, t=TPG)

                def prepare(g, s):
                    if not round_a:
                        dve.wait_ge(R.x_ready, g + 1)
                        tt(vtmp, xg[:, s, :, 0:NV * SH].rearrange("p t (j c) -> p t j c", c=SH), sh_of(s),
                           ALU.mult).then_inc(R.vec, 1)
                    dve.tensor_copy(home[:, s, :], sd[:, s, 24:32])
                    ts(away[:, s, :], sd[:, s, 24:32], -1.0, spare0[:, 1:2], ALU.mult, ALU.add).then_inc(R.step, 1)
                    if not round_a:
                        dve.wait_ge(R.vec, 2 * g + 1)
                        red(xg[:, s, :, 28:32], vtmp, AX, ALU.add).then_inc(R.vec, 1)
                        dve.wait_ge(R.vec, 2 * g + 2)

                def multiply(g, s, k, first):
                    if k == 0 and round_a:
                        dve.wait_ge(R.x_ready, g + 1)
                    dve.wait_ge(R.weights, 4 * g + k + 1)
                    if not (first and k < 2):
                        dve.wait_ge(R.red, 4 * g + k - 1)
                    tt(prod[:, k % 2].rearrange("p t (j i) -> p t j i", i=I),
                       wide[k % 2][:, :, 0:WN].rearrange("p t (j i) -> p t j i", i=I),
                       xg[:, s, k:TPG:4, 12:12 + I].unsqueeze(2).broadcast_to([P, 2, J, I]),
                       ALU.mult).then_inc(R.prod, 1)

                def reduce_(g, s, k):
                    dve.wait_ge(R.prod, 4 * g + k + 1)
                    red(M[:, s % 2, k:TPG:4, 0:J], prod[:, k % 2].rearrange("p t (j i) -> p t j i", i=I),
                        AX, ALU.add).then_inc(R.red, 1)

                def rest(g, s):
                    dve.wait_ge(R.cast, 2 * g + 1)
                    Ms = M[:, s % 2, :, 0:live]
                    tt(Ms, Ms, Mp[:, 0, :, 0:live], ALU.subtract).then_inc(R.rest_left, 1)

                def last_part(g, s):
                    dve.wait_ge(R.cast, 2 * g + 2)
                    tt(Mp[:, 2, :, 0:live], M[:, s % 2, :, 0:live], Mp[:, 1, :, 0:live],
                       ALU.subtract).then_inc(R.parted, 1)

                def targets(g, s):
                    dve.wait_ge(R.out_ready, g + 1)
                    dve.wait_ge(R.out_free, g + 1)
                    ps = banks[2 + s % 2][:, 0:TPG * cols].rearrange("p (t c) -> p t c", c=cols)
                    dve.scalar_tensor_tensor(out=away[:, s, :], in0=ps[:, :, cols - 1], scalar=code_sb[:, 1:2],
                                             in1=away[:, s, :], op0=ALU.is_gt, op1=ALU.mult).then_inc(R.hop, 1)
                    dve.wait_ge(R.hop, g + 1)
                    tt(ui[:, s, :], away[:, s, :], home[:, s, :], ALU.add).then_inc(R.idx_ready, 1)

                def body(it, first, last):
                    for s in range(GPT):
                        g = it * GPT + s
                        f = first and s == 0
                        before = (s - 1) % GPT
                        if not (last and s + 2 >= GPT):
                            build_G(g + 2, (s + 2) % GPT, it + (s + 2) // GPT)
                        prepare(g, s)
                        multiply(g, s, 0, f)
                        if not f:
                            rest(g - 1, before)
                        multiply(g, s, 1, f)
                        reduce_(g, s, 0)
                        if not (first and s < 2):
                            targets(g - 2, (s - 2) % GPT)
                        multiply(g, s, 2, f)
                        reduce_(g, s, 1)
                        if not f:
                            last_part(g - 1, before)
                        multiply(g, s, 3, f)
                        reduce_(g, s, 2)
                        reduce_(g, s, 3)
                        dve.wait_ge(R.red, 4 * g + 4)
                        dve.sem_inc(R.x_free, 1)
                        if round_a:
                            tt(M[:, s % 2, :, 20:32].rearrange("p t (j c) -> p t j c", c=SH),
                               M[:, s % 2, :, 16:20].unsqueeze(3).broadcast_to([P, TPG, NV, SH]), sh_of(s),
                               ALU.mult).then_inc(R.msgs, 1)
                            dve.wait_ge(R.msgs, g + 1)
                        else:
                            dve.sem_inc(R.msgs, 1)
                        dve.sem_inc(R.inputs_free, 1)

                last = dve.memset(ea, 0.0)
                last = dve.memset(Mflat, 1.0)
                last = dve.memset(outflat, 0.0)
                link(last)
                for b in range(2):
                    last = dve.tensor_copy(M[:, b, :, cols - 1], code_sb[:, 0:1].broadcast_to([P, TPG]))
                link(last)
                dve.sem_inc(R.set_up, 1)
                dve.sem_inc(R.x_free, GPT)
                dve.sem_inc(R.inputs_free, GPT)
                build_G(0, 0, 0)
                build_G(1, 1, 0)
                body(0, True, False)
                with dve.Fori(1, TURNS - 1) as it:
                    body(it, False, False)
                body(TURNS - 1, False, True)
                rest(NG - 1, GPT - 1)
                targets(NG - 2, GPT - 2)
                last_part(NG - 1, GPT - 1)
                targets(NG - 1, GPT - 1)

            def add_up(n, st, dst_of, row):
                for q in range(TP):
                    dve.wait_ge(t_in[n], 16 * REPL * (q + 1))
                    for r in range(1, REPL):
                        link(tt(st[0], st[0], st[r], ALU.add))
                    dst_of(q, st[0].rearrange("p (k c) -> p k c", c=row))
                    dve.sem_inc(t_used[n], 1)

            edges(RA, COLS_A, NS, NS + NV)

            Tk = T[:, :].rearrange("p (k c) -> p k c", c=TAB)
            pn = [0]

            def piece_a(q, s_):
                ks = slice(q * KP, (q + 1) * KP)
                rc = rcount[:, ks]
                link(ts(rc, s_[:, :, 28], 1.0, None, ALU.max))
                link(dve.reciprocal(rc, rc))
                link(tt(rc, rc, mask[:, ks], ALU.mult))
                rw = lambda w: rc.unsqueeze(2).broadcast_to([P, KP, w])
                link(tt(Tk[:, ks, 0:12], s_[:, :, NS:NS + 12], rw(12), ALU.mult))
                link(tt(Tk[:, ks, 12:28], s_[:, :, 0:NS], rw(NS), ALU.mult))

            def total(src_, w):
                link(red(stat[:, 0, 0:w], src_.rearrange("p k c -> p c k"), AX, ALU.add))
                dve.sem_inc(part_in, 1)
                pn[0] += 1
                dve.wait_ge(part_sum, pn[0])

            def batch_norm(V, w, first_s, gs, bs, gv):
                sq = sqT[:, 0:K * w].rearrange("p (k c) -> p k c", c=w)
                mean, var, scale = stat[:, 1, 0:w], stat[:, 2, 0:w], stat[:, 3, 0:w]
                S_ = slice(first_s, first_s + NS)
                total(V, w)
                link(ts(mean, banks[0][:, 0:w], 1.0 / N, None, ALU.mult))
                if first_s:
                    link(dve.memset(stat[:, 1, 0:first_s], 0.0))
                link(tt(V, V, per_chan(mean, w), ALU.subtract))
                link(tt(sq, V, V, ALU.mult))
                link(tt(sq, sq, per_node(mask[:, :], w), ALU.mult))
                total(sq, w)
                link(ts(var, banks[0][:, 0:w], 1.0 / N, None, ALU.mult))
                if first_s:
                    link(red(stat[:, 4, 0:NV], stat[:, 2, 0:12].rearrange("p (j c) -> p j c", c=SH), AX, ALU.add))
                    link(ts(stat[:, 4, 0:NV], stat[:, 4, 0:NV], 1.0 / SH, None, ALU.mult))
                    link(dve.tensor_copy(stat[:, 2, 0:12].rearrange("p (j c) -> p j c", c=SH),
                                         stat[:, 4, 0:NV].unsqueeze(2).broadcast_to([P, NV, SH])))
                link(ts(scale, var, EPS, None, ALU.add))
                dve_sqrt(scale)
                link(dve.reciprocal(scale, scale))
                link(tt(stat[:, 3, S_], stat[:, 3, S_], gs, ALU.mult))
                if first_s:
                    link(tt(stat[:, 3, 0:12].rearrange("p (j c) -> p j c", c=SH),
                            stat[:, 3, 0:12].rearrange("p (j c) -> p j c", c=SH),
                            gv.unsqueeze(2).broadcast_to([P, NV, SH]), ALU.mult))
                    link(ts(stat[:, 3, 0:12], stat[:, 3, 0:12], 3.0 ** -0.5, None, ALU.mult))
                link(tt(V, V, per_chan(scale, w), ALU.mult))
                link(tt(V[:, :, S_], V[:, :, S_], per_chan(bs, NS), ALU.add))

            add_up(0, stA, piece_a, ROW_A)
            link(ts(T[:, :], T[:, :], NS ** -0.5, None, ALU.mult))
            batch_norm(Tk, TAB, 12, bn[:, 0:NS], bn[:, NS:2 * NS], bn[:, 4 * NS:4 * NS + NV])
            dve.sem_inc(s_done, 1)
            split(Tk, sqT.rearrange("p (k c) -> p k c", c=TAB), sparts.rearrange("p (k c) -> p k c", c=3 * TAB), TAB)
            dve.sem_inc(s_done, 1)
            dve.wait_ge(s_out, 32)

            edges(RB, COLS_B, NS + NV, NS)
            Vb = T[:, 0:XW].rearrange("p (k c) -> p k c", c=NS)

            def piece_b(q, s_):
                ks = slice(q * KP, (q + 1) * KP)
                link(tt(Vb[:, ks, :], s_, rcount[:, ks].unsqueeze(2).broadcast_to([P, KP, NS]), ALU.mult))

            add_up(1, stB, piece_b, ROW_B)
            link(ts(T[:, 0:XW], T[:, 0:XW], (NS + NV) ** -0.5, None, ALU.mult))
            batch_norm(Vb, NS, 0, bn[:, 2 * NS:3 * NS], bn[:, 3 * NS:4 * NS], None)
            link(tt(xs[:, :], xs[:, :], T[:, 0:XW], ALU.add))
            dve.sem_inc(fin, 1)


NCONST = 18


def lay_out(i):
    f = np.float32
    a = {k: np.asarray(v) for k, v in i.items()}
    N, E = a["x"].shape[0], a["src"].shape[0]
    K = -(-N // (P * 8)) * 8
    NP = P * K
    step = EPG * GPT * PIECES // 4
    EP = -(-E // step) * step
    NG = EP // EPG
    pad = EP - E

    def fill(v, value):
        return np.concatenate([v, np.full((pad,) + v.shape[1:], value, v.dtype)])

    src, dst, typ = fill(a["src"], N), fill(a["dst"], N - 1), fill(a["edge_type_6"], 1)
    if NP == N:
        raise ValueError("needs a padded node")
    cols = lambda v: np.ascontiguousarray(v.reshape(EP // P, P).T)
    vec = fill(a["edge_attr_3"], 0)
    w_t = a["L0_gnn_W"].transpose(2, 0, 1).reshape(8, NT * 8)

    def second(w, b, vec_major):
        w = np.concatenate([w, b[None]])
        wa = w[:, :NS * NS].reshape(-1, NS, NS)
        if vec_major:
            wb = w[:, NS * NS:].reshape(-1, NV, NS)
            full = np.concatenate([wa, wb], 1)
        else:
            wb = w[:, NS * NS:].reshape(-1, NS, NV)
            full = np.concatenate([wa, wb], 2)
        return np.ascontiguousarray(full.transpose(0, 2, 1).reshape(-1, WN))

    def twice(w, rows, columns):
        w = np.pad(w, ((0, rows), (0, columns)))
        z = np.zeros_like(w)
        return np.concatenate([np.concatenate([w, z], 1), np.concatenate([z, w], 1)])

    p = np.arange(P)
    arr = {
        "x": np.concatenate([a["x"], np.zeros((NP - N, NS), f)]).reshape(P, K * NS),
        "src_cols": cols(src), "dst_cols": cols(dst), "typ_cols": cols(typ),
        "vec_cols": np.ascontiguousarray(vec.reshape(EP // P, P, 3).transpose(1, 0, 2).reshape(P, -1)),
        "src_row": src, "dst_row": dst,
        "attr": np.ascontiguousarray(fill(a["edge_attr_48"], 0).T),
        "turn_no": np.tile((np.arange(NG) // GPT).astype(f), (P, 1)),
        "ident": np.eye(P, dtype=f),
        "code": np.stack([3.0 ** (64 - p), 2 * 3.0 ** (64 - p)], 1).astype(f),
        "spare": np.stack([NP // 8 + p, NP + p, p], 1).astype(f),
        "node_mask": (np.arange(NP) < N).astype(f).reshape(P, K),
        "copy_mask": (p[:, None] % NS == np.arange(NS)[None]).astype(f),
        "w_l0": np.repeat(w_t, NS, axis=0),
        "b_l0": a["L0_gnn_Bv"].reshape(-1),
        "w1": np.stack([twice(a[f"L1_gnn_fc{r}_w1"], 64 - H, 64 - H) for r in (0, 1)]),
        "b1": np.stack([np.tile(np.concatenate([a[f"L1_gnn_fc{r}_b1"], np.ones(1, f), np.zeros(63 - H, f)]), 2)
                        for r in (0, 1)])[:, :, None],
        "w2a": twice(second(a["L1_gnn_fc0_w2"], a["L1_gnn_fc0_b2"], False), 63 - H, 0),
        "w2b": twice(second(a["L1_gnn_fc1_w2"], a["L1_gnn_fc1_b2"], True), 63 - H, 0),
        "gs0": a["L1_gnn_bn0_gs"], "bs0": a["L1_gnn_bn0_bs"], "gv0": a["L1_gnn_bn0_gv"],
        "gs1": a["L1_gnn_bn1_gs"], "bs1": a["L1_gnn_bn1_bs"],
    }
    return {k: np.ascontiguousarray(v) for k, v in arr.items()}, N, NG, K


def kernel(**inputs):
    import concourse.bacc as bacc
    from concourse.bass_utils import run_bass_kernel_spmd

    arrays, N, NG, K = lay_out(inputs)
    nc = bacc.Bacc("TRN2", target_bir_lowering=False, num_devices=1)
    aps = {k: nc.dram_tensor("in_" + k, v.shape, mybir.dt.from_np(v.dtype), kind="ExternalInput").ap()
           for k, v in arrays.items()}
    out = nc.dram_tensor("out_x", (P, K * NS), F32, kind="ExternalOutput").ap()
    build(nc, N, NG, out=out, **aps)
    r = run_bass_kernel_spmd(nc, [{"in_" + k: v for k, v in arrays.items()}], core_ids=[0])
    return r.results[0]["out_x"].reshape(P * K, NS)[:N]
```

```python
from contextlib import ExitStack

import numpy as np
import concourse.bass as bass
from concourse import mybir

F32 = mybir.dt.float32
I32 = mybir.dt.int32
U16 = mybir.dt.uint16
BF16 = mybir.dt.bfloat16
ALU = mybir.AluOpType
ACT = mybir.ActivationFunctionType
AX = mybir.AxisListType.X
RMAX = bass.bass_isa.ReduceOp.max

P = 128
TPG = 8
GPT = 4
EPG = P * TPG
REPL = 4
EPS = 1e-5
NS, NV, SH = 16, 4, 3
H = 48
WN = NS * NS + NS * NV
NT = 5
L0 = 8 * NS
ROW_A = 32
ROW_B = NS
COLS_A = 34
COLS_B = NS + 1
LIVE = (COLS_A - 2, COLS_B - 1)
TAB = NV * SH + NS
PIECES = 16
ZW = 1280


def build(nc, N, NG, x, src_cols, dst_cols, typ_cols, vec_cols, src_row, dst_row, attr, turn_no,
          ident, code, spare, columns, node_mask, copy_mask, w_l0, b_l0, w1, b1, w2a, w2b,
          gs0, bs0, gv0, gs1, bs1, out):
    K = x.shape[1] // NS
    NP = P * K
    N0 = N // 8
    K0 = K // 8
    NP0 = P * K0
    TT = NG * TPG
    TURNS = NG // GPT
    PG = NG // PIECES
    XW = K * NS

    def dram(name, shape, dt=F32):
        return nc.dram_tensor(name, shape, dt, kind="Internal").ap()

    z_tab = dram("z_tab", (NP0 * NT, L0))
    z_idx = dram("z_idx", (P, TT), I32)
    side0 = dram("side0", (P, NG * 2 * TPG))
    side = dram("side", (P, NG * 4 * TPG))
    src16 = dram("src16", (NG * EPG,), U16)
    rel16 = dram("rel16", (NG * EPG,), BF16)
    first_d = dram("first_d", (NG,), I32)
    wide_d = dram("wide_d", (NG,), I32)
    h_tab = dram("h_tab", (NP, NS))
    s_tab = dram("s_tab", (NP, TAB))
    h_parts = dram("h_parts", (NP, 3 * NS), BF16)
    s_parts = dram("s_parts", (NP, 3 * TAB), BF16)
    acc0 = [dram(f"acc0_{r}", (NP0 + P, L0)) for r in range(REPL)]
    accA = [dram(f"accA_{r}", (NP + P, ROW_A)) for r in range(REPL)]
    accB = [dram(f"accB_{r}", (NP + P, ROW_B)) for r in range(REPL)]

    with ExitStack() as ctx:
        def sb(name, shape, dt=F32):
            return ctx.enter_context(nc.sbuf_tensor(name, shape, dt))

        def sem(name):
            return ctx.enter_context(nc.semaphore(name))

        xs = sb("xs", [P, XW])
        T = sb("T", [P, K * TAB])
        rcount = sb("rcount", [P, K])
        mask = sb("mask", [P, K])
        small = sb("small", [P, 4, K])
        ident_sb = sb("ident_sb", [P, P])
        ones = sb("ones", [P, P])
        code_sb = sb("code_sb", [P, 2])
        spare0 = sb("spare0", [P, 3])
        cmask = sb("cmask", [P, NS])
        wl = sb("wl", [P, NT * 8])
        bl = sb("bl", [P, NT * 8])
        Mk = sb("Mk", [P, NT * L0])
        w1_sb = [sb(f"w1_{r}", [P, P]) for r in range(2)]
        b1_sb = [sb(f"b1_{r}", [P, 1]) for r in range(2)]
        w2_sb = [sb(f"w2_{r}", [P, 2 * WN]) for r in range(2)]
        bn = sb("bn", [P, 5 * NS])
        stat = sb("stat", [P, 8, 32])
        vmax = sb("vmax", [P, 2])
        last_turn_sb = sb("last_turn_sb", [P, 1], I32)
        first_sb = sb("first_sb", [1, NG], I32)
        wide_sb = sb("wide_sb", [1, NG + 2 * GPT], I32)
        any_wide = sb("any_wide", [1, 1], I32)
        wide_turn = sb("wide_turn", [1, TURNS + 1], I32)
        zero = sb("zero", [P, ZW])
        ARENA = max(20480, K * TAB * 5 // 2, 4 * XW)
        arena = sb("arena", [P, ARENA])

        def carve(sizes):
            views, at = [], 0
            for n in sizes:
                views.append(arena[:, at:at + n])
                at += n
            assert at <= ARENA, at
            return views

        banks = [ctx.enter_context(nc.psum_tensor(f"bank{i}", [P, 512], F32)) for i in range(4)]
        wide = [ctx.enter_context(nc.psum_tensor(f"wide{i}", [P, 2, 512], F32)) for i in range(2)]

        ld_const = sem("ld_const")
        zeroed = sem("zeroed")
        zero_set = sem("zero_set")
        c = sem("dve_step")
        chain = [0]
        sqrt_in = sem("sqrt_in")
        sqrt_out = sem("sqrt_out")
        nsq = [0]

        block = ctx.enter_context(nc.Block())

        def k16(t):
            return t.rearrange("p (k c) -> p k c", c=NS)

        def per_node(v, w):
            return v.unsqueeze(2).broadcast_to([P, K, w])

        def per_chan(v, w):
            return v.unsqueeze(1).broadcast_to([P, K, w])

        def link(ins):
            chain[0] += 1
            ins.then_inc(c, 1)
            nc.vector.wait_ge(c, chain[0])

        def dve_sqrt(ap):
            nsq[0] += 1
            nc.vector.sem_inc(sqrt_in, 1)
            nc.vector.wait_ge(sqrt_out, nsq[0])

        def wait_past(eng, sem_, count):
            if not isinstance(count, int) or count > 0:
                eng.wait_ge(sem_, count)

        ZEACH = (K0 - 1) // PIECES
        ZFIRST = K0 - PIECES * ZEACH

        x_in = sem("x_in")
        h0_done = sem("h0_done")
        zT_done, zTc_done, z_mm, z_sum, z_out = (sem(s) for s in ("zT_done", "zTc_done", "z_mm", "z_sum", "z_out"))
        pc_in, pc_out = ([sem(f"{w}{u}") for u in range(2)] for w in ("pc_in", "pc_out"))
        pc_done = sem("pc_done")
        pc_sq, pc_root = sem("pc_sq"), sem("pc_root")
        psem, qsem = sem("pc_step"), sem("pc_tail")
        bound_in, bound_red, bound_out = sem("bound_in"), sem("bound_red"), sem("bound_out")
        l0_done = sem("l0_done")
        wide_idx, wide_rows, wide_in, wide_max, row_in = (
            sem(s) for s in ("wide_idx", "wide_rows", "wide_in", "wide_max", "row_in"))
        paced, zh_done = sem("paced"), sem("zh_done")
        y_in, y_used = sem("y_in"), sem("y_used")
        h1_done, h1_out = sem("h1_done"), sem("h1_out")
        rA_done, rB_done = sem("rA_done"), sem("rB_done")
        t_in = [sem("tA_in"), sem("tB_in")]
        t_used = [sem("tA_used"), sem("tB_used")]
        part_in, part_sum = sem("part_in"), sem("part_sum")
        s_done, s_out = sem("s_done"), sem("s_out")
        fin, fin_out = sem("fin"), sem("fin_out")

        ZMEM = XW + 2 * P + 2 * NT * L0
        d_p, _, h_p, zTs, zh, zts, bias_row = carve([XW, ARENA - XW - ZMEM, XW, P, P, NT * L0, NT * L0])
        bias_row = bias_row[0:1, :]
        W8 = PG * TPG
        inner = [3 * W8, W8, W8, W8]
        through = [W8, W8, W8, 3 * W8, 4 * W8, 2 * W8, W8, PG, EPG, EPG, EPG // 2, EPG // 2, 8]
        assert sum(inner) + 2 * sum(through) <= ARENA - ZMEM
        v = carve(inner + 2 * through)
        shp, rootp, t1p, t2p = v[:4]

        class Piece:

            def __init__(b, views):
                b.src, b.dst, b.typ, b.vec, b.side, b.side0, b.zi, b.turn, b.srow, b.drow, b.src16, b.rel16, b.stat = views
                b.src, b.dst, b.typ, b.zi = (t.bitcast(I32) for t in (b.src, b.dst, b.typ, b.zi))
                b.srow, b.drow = b.srow.bitcast(I32), b.drow.bitcast(I32)
                b.src16, b.rel16 = b.src16.bitcast(U16), b.rel16.bitcast(BF16)
                b.first, b.wide = b.stat[:, 4:5].bitcast(I32), b.stat[:, 5:6].bitcast(I32)

        n = len(through)
        pieces = [Piece(v[4:4 + n]), Piece(v[4 + n:])]

        v = carve([GPT * EPG, GPT * TPG * (L0 + 1), GPT * TPG * L0, 2 * EPG, GPT * TPG, GPT * 2 * TPG, GPT * TPG, TPG,
                   NG, NG, P, TPG])
        rowb0 = v[0].bitcast(I32).rearrange("p (s e) -> p s e", s=GPT)
        zb = v[1].rearrange("p (s t c) -> p s t c", s=GPT, t=TPG)
        out0 = v[2].rearrange("p (s t c) -> p s t c", s=GPT, t=TPG)
        S0 = v[3].rearrange("p (s e) -> p s e", s=2)
        zi = v[4].bitcast(I32).rearrange("p (s t) -> p s t", s=GPT)
        sd0 = v[5].rearrange("p (s t) -> p s t", s=GPT)
        ui0 = v[6].bitcast(I32).rearrange("p (s t) -> p s t", s=GPT)
        tmp0 = v[7]
        first_i, first0 = v[8].bitcast(I32), v[9]
        columns_sb = v[10]
        rel0 = v[11]

        PT = 3 * TPG
        v = carve([GPT * EPG // 2, GPT * EPG // 2, GPT * EPG // 2, GPT * TPG * 32, 2 * 2 * WN, EPG, EPG, EPG,
                   2 * TPG * COLS_A, 3 * TPG * COLS_A, GPT * TPG * ROW_A, TPG, GPT * 4 * TPG, GPT * TPG, GPT * TPG,
                   GPT * TPG, TPG * NV * SH, GPT * 3 * TAB // 2, EPG])
        srow16 = v[0].bitcast(U16).rearrange("p (s e) -> p s e", s=GPT)
        drow16 = v[1].bitcast(BF16).rearrange("p (s e) -> p s e", s=GPT)
        ea = v[2].rearrange("p (s e) -> p s e", s=GPT)
        xg = v[3].rearrange("p (s t c) -> p s t c", s=GPT, t=TPG)
        prod = v[4].rearrange("p (s t w) -> p s t w", s=2, t=2)
        Sm = v[5].bitcast(BF16).rearrange("p (s e) -> p s e", s=2)
        hT = v[6].rearrange("p (s e) -> p s e", s=2)
        G = v[7].bitcast(BF16).rearrange("p (s e) -> p s e", s=2)
        Mflat = v[8]
        Mparts = v[9].bitcast(BF16)
        outflat = v[10]
        di = v[11].bitcast(I32)
        sd = v[12].rearrange("p (s t) -> p s t", s=GPT)
        ui = v[13].bitcast(I32).rearrange("p (s t) -> p s t", s=GPT)
        away = v[14].rearrange("p (s t) -> p s t", s=GPT)
        home = v[15].rearrange("p (s t) -> p s t", s=GPT)
        vtmp = v[16].rearrange("p (t j c) -> p t j c", j=NV, c=SH)
        window = v[17].bitcast(BF16).rearrange("p (s c) -> p s c", s=GPT)
        dist = v[18]

        y_st = carve([XW] * REPL)
        TP = 4
        KP = K // TP
        stA = carve([KP * ROW_A] * REPL)
        stB = carve([KP * ROW_B] * REPL)
        sqT = carve([K * TAB])[0]
        nb = carve([XW, XW, 3 * XW // 2])
        hparts = nb[2].bitcast(BF16)
        sparts = carve([K * TAB, 3 * K * TAB // 2])[1].bitcast(BF16)

        class EdgeLoop:

            def __init__(r, name, n):
                r.n = n
                r.ld_rest = [sem(f"{name}_rest{s}") for s in range(GPT)]
                r.rest = 16 * (6 if n else 2)
                r.summed = [sem(f"{name}_summed{q}") for q in range(REPL)]
                r.inputs_free = sem(name + "_inputs_free")
                r.x_free = sem(name + "_x_free")
                r.out_free = sem(name + "_out_free")
                r.S_built = sem(name + "_S_built")
                r.joined = sem(name + "_joined")
                r.out_ready = sem(name + "_out_ready")
                r.idx_ready = sem(name + "_idx_ready")
                r.set_up = sem(name + "_set_up")
                r.step = sem(name + "_step")
                if n == 0:
                    r.ld_idx = [sem(f"{name}_idx{s}") for s in range(GPT)]
                    r.gathered = [sem(f"{name}_gathered{s}") for s in range(GPT)]
                    return
                r.G_built = sem(name + "_G_built")
                r.picked = sem(name + "_picked")
                r.x_copied = sem(name + "_x_copied")
                r.x_ready = sem(name + "_x_ready")
                r.cast = sem(name + "_cast")
                r.rest_left = sem(name + "_rest_left")
                r.parted = sem(name + "_parted")
                r.hop = sem(name + "_hop")
                r.rows_free = sem(name + "_rows_free")
                r.hid = sem(name + "_hid")
                r.relu = sem(name + "_relu")
                r.weights = sem(name + "_weights")
                r.prod = sem(name + "_prod")
                r.red = sem(name + "_red")
                r.vec = sem(name + "_vec")
                r.squared = sem(name + "_squared")
                r.msgs = sem(name + "_msgs")

        R0, RA, RB = EdgeLoop("l0", 0), EdgeLoop("a", 1), EdgeLoop("b", 2)

        @block.sync
        def _(sp):
            sp.dma_start(xs[:, :], x).then_inc(x_in, 16)
            n = 0
            for dst_, src_ in ((ident_sb[:, :], ident), (code_sb[:, :], code), (spare0[:, :], spare),
                               (mask[:, :], node_mask), (cmask[:, :], copy_mask), (wl[:, :], w_l0),
                               (bl[:, :], b_l0.partition_broadcast(P)), (w1_sb[0][:, :], w1[0]),
                               (w1_sb[1][:, :], w1[1]), (b1_sb[0][:, :], b1[0]), (b1_sb[1][:, :], b1[1]),
                               (w2_sb[0][:, :], w2a), (w2_sb[1][:, :], w2b),
                               (bn[:, 0:NS], gs0.partition_broadcast(P)), (bn[:, NS:2 * NS], bs0.partition_broadcast(P)),
                               (bn[:, 2 * NS:3 * NS], gs1.partition_broadcast(P)),
                               (bn[:, 3 * NS:4 * NS], bs1.partition_broadcast(P)),
                               (bn[:, 4 * NS:4 * NS + NV], gv0.partition_broadcast(P))):
                sp.dma_start(dst_, src_).then_inc(ld_const, 16)
                n += 1
            assert n == NCONST

            sp.wait_ge(h0_done, 1)

            src_rows = src_row.rearrange("(g e) -> g e", e=EPG)
            dst_rows = dst_row.rearrange("(g e) -> g e", e=EPG)

            def load(q, u):
                b = pieces[u]
                wait_past(sp, pc_done, q - 1)
                sp.dma_start(b.src, src_cols[:, bass.ds(q * W8, W8)]).then_inc(pc_in[u], 16)
                sp.dma_start(b.dst, dst_cols[:, bass.ds(q * W8, W8)]).then_inc(pc_in[u], 16)
                sp.dma_start(b.typ, typ_cols[:, bass.ds(q * W8, W8)]).then_inc(pc_in[u], 16)
                sp.dma_start(b.vec, vec_cols[:, bass.ds(q * 3 * W8, 3 * W8)]).then_inc(pc_in[u], 16)
                sp.dma_start(b.turn, turn_no[:, bass.ds(q * PG, PG)]).then_inc(pc_in[u], 16)
                sp.dma_start(b.srow[0:PG, :], src_rows[bass.ds(q * PG, PG), :]).then_inc(pc_in[u], 16)
                sp.dma_start(b.drow[0:PG, :], dst_rows[bass.ds(q * PG, PG), :]).then_inc(pc_in[u], 16)

            def store(q, u):
                b = pieces[u]
                sp.wait_ge(pc_done, q + 1)
                sp.dma_start(side[:, bass.ds(q * 4 * W8, 4 * W8)], b.side).then_inc(pc_out[u], 16)
                sp.dma_start(side0[:, bass.ds(q * 2 * W8, 2 * W8)], b.side0).then_inc(pc_out[u], 16)
                sp.dma_start(z_idx[:, bass.ds(q * W8, W8)], b.zi).then_inc(pc_out[u], 16)
                sp.dma_start(src16.rearrange("(g e) -> g e", e=EPG)[bass.ds(q * PG, PG), :], b.src16[0:PG, :]).then_inc(pc_out[u], 16)
                sp.dma_start(rel16.rearrange("(g e) -> g e", e=EPG)[bass.ds(q * PG, PG), :], b.rel16[0:PG, :]).then_inc(pc_out[u], 16)
                sp.dma_start(first_d.unsqueeze(1)[bass.ds(q * PG, PG), :], b.first[0:PG, :]).then_inc(pc_out[u], 16)
                sp.dma_start(wide_d.unsqueeze(1)[bass.ds(q * PG, PG), :], b.wide[0:PG, :]).then_inc(pc_out[u], 16)

            def load_store(q, last):
                load(q + 1, 1)
                store(q, 0)
                if not last:
                    load(q + 2, 0)
                store(q + 1, 1)

            load(0, 0)
            load_store(0, False)
            with sp.Fori(1, PIECES // 2 - 1) as h:
                load_store(h * 2, False)
            load_store(PIECES - 2, True)
            for u in range(2):
                sp.wait_ge(pc_out[u], 112 * (PIECES // 2))
            sp.dma_start(first_sb[:, :], first_d.unsqueeze(0)).then_inc(row_in, 16)
            sp.dma_start(wide_sb[:, 0:NG], wide_d.unsqueeze(0)).then_inc(wide_in, 16)
            sp.dma_start(first_i, first_d.partition_broadcast(P)).then_inc(wide_in, 16)
            sp.dma_start(columns_sb, columns).then_inc(wide_in, 16)

            sp.wait_ge(bound_out, 1)
            turns = sp.value_load(last_turn_sb[0:1, 0:1], min_val=2, max_val=TURNS - 1) + 1

            def inputs0(it, wide):
                for s in range(GPT):
                    g = it * GPT + s
                    sp.wait_ge(R0.inputs_free, g + 1)
                    sp.dma_start(zi[:, s, :], z_idx[:, bass.ds(g * TPG, TPG)]).then_inc(R0.ld_idx[s], 16)
                    sp.dma_start(sd0[:, s, :], side0[:, bass.ds(g * 2 * TPG, 2 * TPG)]).then_inc(R0.ld_rest[s], 16)
                    if wide:
                        sp.dma_start(rowb0[:, s, :], dst_row[bass.ds(g * EPG, EPG)].partition_broadcast(P)).then_inc(R0.ld_rest[s], 16)

            sp.wait_ge(R0.set_up, 1)
            with sp.If(sp.value_load(any_wide[0:1, 0:1], min_val=0, max_val=1) > 0):
                with sp.Fori(0, turns) as it:
                    inputs0(it, True)
            with sp.Else():
                with sp.Fori(0, turns) as it:
                    inputs0(it, False)

            sp.wait_ge(l0_done, 1)
            for r in range(REPL):
                sp.dma_start(y_st[r], acc0[r][0:NP0, :].rearrange("(p k) c -> p (k c)", p=P)).then_inc(y_in, 16)
            sp.wait_ge(h1_done, 1)
            sp.dma_start(h_tab.rearrange("(p k) c -> p (k c)", p=P), nb[0]).then_inc(h1_out, 16)
            sp.wait_ge(h1_done, 2)
            sp.dma_start(h_parts.rearrange("(p k) c -> p (k c)", p=P), hparts).then_inc(h1_out, 16)
            sp.wait_ge(h1_out, 32)

            sp.wait_ge(row_in, 16)

            HE = EPG // 2

            def feed(R, tab, width):
                with sp.Fori(0, TURNS) as it:
                    for s in range(GPT):
                        g = it * GPT + s
                        first = sp.value_load(first_sb[0:1, bass.ds(g, 1)], min_val=0, max_val=NP - P)
                        sp.wait_ge(R.inputs_free, g + 1)
                        sp.wait_ge(R.rows_free, g + 1)
                        for j in range(2):
                            sp.dma_start(ea[64 * j:64 * j + H, s, :], attr[:, bass.ds(g * EPG + j * HE, HE)]).then_inc(R.ld_rest[s], 16)
                        sp.dma_start(srow16[:, s, :], src16[bass.ds(g * EPG, EPG)].partition_broadcast(P)).then_inc(R.ld_rest[s], 16)
                        sp.dma_start(drow16[:, s, :], rel16[bass.ds(g * EPG, EPG)].partition_broadcast(P)).then_inc(R.ld_rest[s], 16)
                        sp.dma_start(sd[:, s, :], side[:, bass.ds(g * 4 * TPG, 4 * TPG)]).then_inc(R.ld_rest[s], 16)
                        sp.dma_start(window[:, s, 0:3 * width], tab[bass.ds(first, P), :]).then_inc(R.ld_rest[s], 16)

            def tables(R, acc, st, row, n):
                for q in range(TP):
                    if q:
                        sp.wait_ge(t_used[n], q)
                    for r in range(REPL):
                        sp.dma_start(st[r], acc[r][0:NP, :].rearrange("(p k) c -> p (k c)", p=P)
                                     [:, q * KP * row:(q + 1) * KP * row]).then_inc(t_in[n], 16)

            feed(RA, h_parts, NS)
            sp.wait_ge(rA_done, 1)
            tables(RA, accA, stA, ROW_A, 0)
            sp.wait_ge(s_done, 1)
            sp.dma_start(s_tab.rearrange("(p k) c -> p (k c)", p=P), T[:, :]).then_inc(s_out, 16)
            sp.wait_ge(s_done, 2)
            sp.dma_start(s_parts.rearrange("(p k) c -> p (k c)", p=P), sparts).then_inc(s_out, 16)
            sp.wait_ge(s_out, 32)
            feed(RB, s_parts, TAB)
            sp.wait_ge(rB_done, 1)
            tables(RB, accB, stB, ROW_B, 1)
            sp.wait_ge(fin, 1)
            sp.dma_start(out, xs[:, :]).then_inc(fin_out, 16)
            sp.wait_ge(fin_out, 16)

        @block.gpsimd
        def _(pool):
            last_row = {rows: pool.to_reg(rows - 1) for rows in sorted({NP0 * NT, NP, NP0 + P, NP + P})}

            def gather(dst_, tab, idx, signal):
                pool.indirect_dma_start(out=dst_, out_offset=None, in_=tab,
                                        in_offset=bass.IndirectOffsetOnAxis(ap=idx, axis=0),
                                        bounds_check=last_row[tab.shape[0]], oob_is_err=True).then_inc(signal, 16)

            def add_rows(tab, src_, idx, signal):
                pool.indirect_dma_start(out=tab, out_offset=bass.IndirectOffsetOnAxis(ap=idx, axis=0),
                                        in_=src_, in_offset=None, bounds_check=last_row[tab.shape[0]],
                                        oob_is_err=True, compute_op=ALU.add).then_inc(signal, 16)

            pool.wait_ge(zero_set, 1)
            n = 0
            for acc in acc0 + accA + accB:
                flat = acc.rearrange("(p k) c -> p (k c)", p=P)
                w = flat.shape[1]
                for a in range(0, w, ZW):
                    b = min(w, a + ZW)
                    pool.dma_start(flat[:, a:b], zero[:, 0:b - a]).then_inc(zeroed, 16)
                    n += 1
            pool.wait_ge(zeroed, 16 * n)

            pool.wait_ge(bound_in, 1)
            pool.partition_all_reduce(vmax[:, 1:2], vmax[:, 0:1], P, RMAX).then_inc(bound_red, 1)
            pool.wait_ge(bound_red, 1)
            pool.tensor_copy(last_turn_sb[:, :], vmax[:, 1:2]).then_inc(bound_out, 1)
            pool.wait_ge(bound_out, 1)
            last_turn = pool.value_load(last_turn_sb[0:1, 0:1], min_val=2, max_val=TURNS - 1)

            R = R0
            pool.wait_ge(z_out, 16 * K0)

            def scatter(R, g, s, acc, rows, idx, between):
                pool.wait_ge(R.out_ready, g + 1)
                pool.wait_ge(R.idx_ready, g + 1)
                for t in range(TPG):
                    wait_past(pool, R.summed[t % REPL], 16 * (TPG // REPL) * g + 16 * (t // REPL))
                    pool.sem_inc(paced, 1)
                    add_rows(acc[t % REPL], rows[:, s, t, :], idx[:, s, t:t + 1], R.summed[t % REPL])
                    between(t)
                pool.sem_inc(R.out_free, 1)

            def fetch0_waits(g, s, turn):
                pool.wait_ge(R.ld_idx[s], 16 * turn + 16)
                pool.wait_ge(R.x_free, g + 1)
                pool.sem_inc(paced, 1)

            def fetch0(s, t):
                gather(zb[:, s, t, 0:L0], z_tab, zi[:, s, t:t + 1], R.gathered[s])

            def body0(it, last):
                for s in range(GPT):
                    g = it * GPT + s
                    ahead = (s + 2) % GPT
                    more = not (last and s + 2 >= GPT)
                    if more:
                        fetch0_waits(g + 2, ahead, it + (s + 2) // GPT)
                    scatter(R, g, s, acc0, out0, ui0, lambda t: fetch0(ahead, t) if more else None)

            def body0_window(it, first, last):
                for s in range(GPT):
                    g = it * GPT + s
                    ahead = (s + 2) % GPT
                    more = not (last and s + 2 >= GPT)
                    if more:
                        fetch0_waits(g + 2, ahead, it + (s + 2) // GPT)
                        for t in range(TPG // 2):
                            fetch0(ahead, t)
                    pool.wait_ge(R.out_ready, g + 1)
                    pool.wait_ge(R.idx_ready, g + 1)
                    pool.sem_inc(paced, 1)
                    add_rows(acc0[s], out0[:, s, 0, :], ui0[:, s, 0:1], R.summed[s])
                    if more:
                        for t in range(TPG // 2, TPG):
                            fetch0(ahead, t)
                    if not (first and s < GPT - 1):
                        pool.wait_ge(R.summed[(s + 1) % GPT], 16 * (it + (s + 1) // GPT))
                    pool.sem_inc(R.out_free, 1)

            pool.wait_ge(R.set_up, 1)
            for g in range(2):
                fetch0_waits(g, g, 0)
                for t in range(TPG):
                    fetch0(g, t)
            with pool.If(pool.value_load(any_wide[0:1, 0:1], min_val=0, max_val=1) > 0):
                pool.sem_inc(R.out_free, GPT - 1)
                body0(0, False)
                with pool.Fori(1, last_turn) as it:
                    body0(it, False)
                body0(last_turn, True)
                for r in range(REPL):
                    pool.wait_ge(R.summed[r], 16 * (TPG // REPL) * GPT * (last_turn + 1))
            with pool.Else():
                pool.sem_inc(R.out_free, 1)
                body0_window(0, True, False)
                with pool.Fori(1, last_turn) as it:
                    body0_window(it, False, False)
                body0_window(last_turn, False, True)
                for r in range(REPL):
                    pool.wait_ge(R.summed[r], 16 * (last_turn + 1))
            pool.sem_inc(l0_done, 1)

            def edges(R, tab, width, acc, row, xcols):
                rows = outflat.rearrange("p (s t c) -> p s t c", s=GPT, t=TPG)[:, :, :, 0:row]

                def hand_over(g, s, wide):
                    pool.wait_ge(R.x_copied, g + 1)
                    pool.sem_inc(paced, 1)
                    with pool.If(wide > 0):
                        pool.reg_add(fetched, fetched, 1)
                        n = pool.snap(fetched, min_val=1, max_val=2 * NG)
                        pool.dma_start(di, dst_cols[:, bass.ds(g * TPG, TPG)]).then_inc(wide_idx, 16)
                        pool.wait_ge(wide_idx, 16 * n)
                        pool.sem_inc(paced, 1)
                        for t in range(TPG):
                            gather(xg[:, s, t, xcols:xcols + width], tab, di[:, t:t + 1], wide_rows)
                        pool.wait_ge(wide_rows, 16 * TPG * n)
                        pool.sem_inc(paced, 1)
                    pool.sem_inc(R.x_ready, 1)

                def body(it, last):
                    wide = pool.value_load(wide_turn[0:1, bass.ds(it + 1, 1)], min_val=0, max_val=1)
                    for s in range(GPT):
                        g = it * GPT + s
                        if not (last and s + 3 >= GPT):
                            hand_over(g + 3, (s + 3) % GPT, wide)
                        scatter(R, g, s, acc, rows, ui, lambda t: None)

                pool.sem_inc(R.out_free, GPT - 1)
                wide = pool.value_load(wide_turn[0:1, 0:1], min_val=0, max_val=1)
                for g in range(3):
                    hand_over(g, g, wide)
                body(0, False)
                with pool.Fori(1, TURNS - 1) as it:
                    body(it, False)
                body(TURNS - 1, True)
                for r in range(REPL):
                    pool.wait_ge(R.summed[r], 16 * (TPG // REPL) * NG)

            pool.wait_ge(wide_max, 1)
            fetched = pool.alloc_register("fetched")
            pool.reg_mov(fetched, 0)
            pool.wait_ge(h1_out, 32)
            edges(RA, h_tab, NS, accA, ROW_A, 12)
            pool.sem_inc(rA_done, 1)
            pool.wait_ge(s_out, 32)
            edges(RB, s_tab, TAB, accB, ROW_B, 0)
            pool.sem_inc(rB_done, 1)

        @block.tensor
        def _(pe):
            pe.wait_ge(h0_done, 1)
            pe.wait_ge(ld_const, 16 * NCONST)

            half = NT * L0 // 2

            def z_tile(k):
                wait_past(pe, zTc_done, k)
                pe.wait_ge(zh_done, k + 1)
                pe.transpose(banks[0][:, 0:P], zh, ident_sb[:, :]).then_inc(zT_done, 1)
                pe.wait_ge(zTc_done, k + 1)
                wait_past(pe, z_sum, 2 * k)
                for i in range(2):
                    pe.matmul(banks[1 + i][:, 0:half], zTs, Mk[:, i * half:(i + 1) * half], start=True, stop=False)
                    pe.matmul(banks[1 + i][:, 0:half], ones[0:1, :], bias_row[:, i * half:(i + 1) * half],
                              start=False, stop=True).then_inc(z_mm, 1)

            z_tile(0)
            with pe.Fori(1, K0) as k:
                z_tile(k)

            pe.wait_ge(bound_out, 1)
            turns = pe.value_load(last_turn_sb[0:1, 0:1], min_val=2, max_val=TURNS - 1) + 1
            R = R0

            def join0(it):
                for s in range(GPT):
                    g = it * GPT + s
                    pe.wait_ge(R.gathered[s], 16 * TPG * it + 16 * TPG)
                    pe.wait_ge(R.S_built, g + 1)
                    wait_past(pe, R.idx_ready, g)
                    for t in range(TPG):
                        last = pe.matmul(banks[t // 3][:, (t % 3) * (L0 + 1):(t % 3 + 1) * (L0 + 1)],
                                         S0[:, s % 2, t * P:(t + 1) * P], zb[:, s, t, :], start=True, stop=True)
                    last.then_inc(R.joined, 1)

            def sum0_window(it):
                for s in range(GPT):
                    g = it * GPT + s
                    pe.wait_ge(R.gathered[s], 16 * TPG * it + 16 * TPG)
                    pe.wait_ge(R.S_built, g + 1)
                    wait_past(pe, R.out_ready, g - 1)
                    for t in range(TPG):
                        last = pe.matmul(banks[s % 2][:, 0:L0], S0[:, s % 2, t * P:(t + 1) * P], zb[:, s, t, 0:L0],
                                         start=(t == 0), stop=(t == TPG - 1))
                    last.then_inc(R.joined, 1)

            pe.wait_ge(R.set_up, 1)
            with pe.If(pe.value_load(any_wide[0:1, 0:1], min_val=0, max_val=1) > 0):
                join0(0)
                with pe.Fori(1, turns) as it:
                    join0(it)
            with pe.Else():
                sum0_window(0)
                with pe.Fori(1, turns) as it:
                    sum0_window(it)

            def edges(R, cols, width):
                r = R.n - 1
                live = LIVE[r]
                Mp = Mparts[:, 0:3 * TPG * cols].rearrange("p (q t c) -> p q t c", q=3, t=TPG)

                def hidden(g, s, turn):
                    pe.wait_ge(R.ld_rest[s], R.rest * turn + R.rest)
                    wait_past(pe, R.relu, g)
                    pe.matmul(banks[0][:, :], w1_sb[r][:, :], ea[:, s, :],
                              start=True, stop=True).then_inc(R.hid, 1)

                def pick(g, s):
                    pe.wait_ge(R.G_built, g + 1)
                    wait_past(pe, R.x_copied, g)
                    for t in range(TPG):
                        for q in range(3):
                            last = pe.matmul(banks[1][:, t * width:(t + 1) * width], G[:, s % 2, t * P:(t + 1) * P],
                                             window[:, s, q * width:(q + 1) * width], start=(q == 0), stop=(q == 2))
                    last.then_inc(R.picked, 1)

                def weights(g, s, k, first=False):
                    pe.wait_ge(R.relu, g + 1)
                    if not (first and k < 2):
                        pe.wait_ge(R.prod, 4 * g + k - 1)
                    for j in range(2):
                        last = pe.matmul(wide[k % 2][:, j, 0:WN], hT[:, s % 2, k * P:(k + 1) * P],
                                         w2_sb[r][:, j * WN:(j + 1) * WN], start=True, stop=True)
                    last.then_inc(R.weights, 1)

                def join(g, s):
                    pe.wait_ge(R.parted, g + 1)
                    pe.wait_ge(R.S_built, g + 1)
                    wait_past(pe, R.idx_ready, g - 1)
                    for t in range(TPG):
                        for q in range(3):
                            w = cols if q == 0 else live
                            last = pe.matmul(banks[2 + s % 2][:, t * cols:t * cols + w], Sm[:, s % 2, t * P:(t + 1) * P],
                                             Mp[:, q, t, 0:w], start=(q == 0), stop=(q == 2))
                    last.then_inc(R.joined, 1)

                def body(it, first, last):
                    for s in range(GPT):
                        g = it * GPT + s
                        f = first and s == 0
                        weights(g, s, 0, f)
                        weights(g, s, 1, f)
                        if not (last and s == GPT - 1):
                            hidden(g + 1, (s + 1) % GPT, it + (s + 1) // GPT)
                        weights(g, s, 2)
                        if not (last and s + 2 >= GPT):
                            pick(g + 2, (s + 2) % GPT)
                        weights(g, s, 3)
                        if not f:
                            join(g - 1, (s - 1) % GPT)

                pe.wait_ge(R.set_up, 1)
                pick(0, 0)
                hidden(0, 0, 0)
                pick(1, 1)
                body(0, True, False)
                with pe.Fori(1, TURNS - 1) as it:
                    body(it, False, False)
                body(TURNS - 1, False, True)
                join(NG - 1, GPT - 1)

            def totals():
                for i in range(2):
                    totals.n += 1
                    pe.wait_ge(part_in, totals.n)
                    pe.matmul(banks[0][:, 0:32], ones[:, :], stat[:, 0, :], start=True, stop=True).then_inc(part_sum, 1)
            totals.n = 0

            edges(RA, COLS_A, NS)
            totals()
            edges(RB, COLS_B, TAB)
            totals()

        @block.scalar
        def _(act):
            def root(ap, bias_done, signal_done):
                act.wait_ge(sqrt_in, bias_done)
                act.activation(ap, ap, ACT.Sqrt).then_inc(signal_done, 1)

            root(small[:, 1, :], 1, sqrt_out)
            act.wait_ge(h0_done, 1)

            def z_copies(k):
                wait_past(act, zT_done, k)
                act.copy(zh, h_p[:, bass.ds(k * P, P)]).then_inc(zh_done, 1)
                act.wait_ge(zT_done, k + 1)
                wait_past(act, z_mm, 2 * k)
                act.copy(zTs, banks[0][:, 0:P]).then_inc(zTc_done, 1)

            z_rows = z_tab.rearrange("(p k t) c -> p k (t c)", p=P, t=NT)
            half = NT * L0 // 2

            def z_leave(k):
                wait_past(act, z_out, 16 * k)
                for i in range(2):
                    act.wait_ge(z_mm, 2 * k + i + 1)
                    act.copy(zts[:, i * half:(i + 1) * half], banks[1 + i][:, 0:half]).then_inc(z_sum, 1)
                act.wait_ge(z_sum, 2 * k + 2)
                act.dma_start(z_rows[:, bass.ds(k, 1), :].rearrange("p a c -> p (a c)"), zts).then_inc(z_out, 16)

            for k in range(ZFIRST):
                z_copies(k)
                z_leave(k)
            with act.Fori(0, PIECES) as q:
                act.wait_ge(pc_sq, q + 1)
                act.activation(rootp, rootp, ACT.Sqrt).then_inc(pc_root, 1)
                for j in range(ZEACH):
                    z_copies(q * ZEACH + (ZFIRST + j))
                    z_leave(q * ZEACH + (ZFIRST + j))

            act.wait_ge(bound_out, 1)
            turns = act.value_load(last_turn_sb[0:1, 0:1], min_val=2, max_val=TURNS - 1) + 1
            R = R0

            def out_copies(it, wide):
                for s in range(GPT):
                    g = it * GPT + s
                    act.wait_ge(R.joined, g + 1)
                    act.wait_ge(R.out_free, g + 1)
                    if wide:
                        for b in range(3):
                            n = min(3, TPG - 3 * b)
                            last = act.copy(out0[:, s, 3 * b:3 * b + n, :],
                                            banks[b][:, 0:n * (L0 + 1)].rearrange("p (t c) -> p t c", c=L0 + 1)[:, :, 0:L0])
                    else:
                        last = act.copy(out0[:, s, 0, :], banks[s % 2][:, 0:L0])
                    last.then_inc(R.out_ready, 1)

            act.wait_ge(R.set_up, 1)
            with act.If(act.value_load(any_wide[0:1, 0:1], min_val=0, max_val=1) > 0):
                with act.Fori(0, turns) as it:
                    out_copies(it, True)
            with act.Else():
                with act.Fori(0, turns) as it:
                    out_copies(it, False)
            root(small[:, 1, :], 2, sqrt_out)

            def edges(R, cols, row, width, xcols):
                r = R.n - 1
                live = LIVE[r]
                outv = outflat.rearrange("p (s t c) -> p s t c", s=GPT, t=TPG)

                Mp = Mparts[:, 0:3 * TPG * cols].rearrange("p (q t c) -> p q t c", q=3, t=TPG)
                M = Mflat[:, 0:2 * TPG * cols].rearrange("p (s t c) -> p s t c", s=2, t=TPG)

                def relu(g, s, first=False):
                    act.wait_ge(R.hid, g + 1)
                    if not first:
                        act.wait_ge(R.weights, 4 * g - 4)
                    act.activation(hT[:, s % 2, :], banks[0][:, :], ACT.Relu, bias=b1_sb[r][:, :]).then_inc(R.relu, 1)

                def part(g, s, q):
                    if q == 0:
                        act.wait_ge(R.msgs, g + 1)
                        wait_past(act, R.joined, g)
                    else:
                        act.wait_ge(R.rest_left, g + 1)
                    w = cols if q == 0 else live
                    act.copy(Mp[:, q, :, 0:w], M[:, s % 2, :, 0:w]).then_inc(R.cast, 1)

                def distances(g, s, turn, t0):
                    act.wait_ge(R.ld_rest[s], R.rest * turn + R.rest)
                    wait_past(act, R.S_built, g)
                    for t in range(t0, t0 + 4):
                        last = act.activation(dist[:, t * P:(t + 1) * P], srow16[:, s, t * P:(t + 1) * P], ACT.Square,
                                              scale=-1.0, bias=sd[:, s, 24 + t:25 + t])
                    last.then_inc(R.squared, 1)

                def build_S(g, s):
                    act.wait_ge(R.squared, 2 * g + 2)
                    act.sem_inc(R.rows_free, 1)
                    wait_past(act, R.joined, g - 1)
                    act.activation(Sm[:, s % 2, :], dist, ACT.Relu, scale=-2.0, bias=ones[:, 0:1]).then_inc(R.S_built, 1)

                def copy_rows(g, s):
                    act.wait_ge(R.picked, g + 1)
                    act.wait_ge(R.x_free, g + 1)
                    act.copy(xg[:, s, :, xcols:xcols + width],
                             banks[1][:, 0:TPG * width].rearrange("p (t c) -> p t c", c=width)).then_inc(R.x_copied, 1)

                def copy_out(g, s):
                    act.wait_ge(R.joined, g + 1)
                    act.wait_ge(R.out_free, g + 1)
                    ps = banks[2 + s % 2][:, 0:TPG * cols].rearrange("p (t c) -> p t c", c=cols)
                    last = act.copy(outv[:, s, :, 0:NS], ps[:, :, 0:NS])
                    if row == ROW_A:
                        last = act.copy(outv[:, s, :, NS:NS + 13], ps[:, :, 20:33])
                    last.then_inc(R.out_ready, 1)

                def body(it, first, last):
                    for s in range(GPT):
                        g = it * GPT + s
                        f = first and s == 0
                        if not f:
                            part(g - 1, (s - 1) % GPT, 0)
                        if not (first and s < 2):
                            copy_out(g - 2, (s - 2) % GPT)
                        distances(g, s, it, 0)
                        if not f:
                            part(g - 1, (s - 1) % GPT, 1)
                        if not (last and s == GPT - 1):
                            relu(g + 1, (s + 1) % GPT, f)
                        distances(g, s, it, 4)
                        if not (last and s + 2 >= GPT):
                            copy_rows(g + 2, (s + 2) % GPT)
                        build_S(g, s)

                act.sem_inc(R.rows_free, GPT)
                act.wait_ge(R.set_up, 1)
                copy_rows(0, 0)
                relu(0, 0, True)
                copy_rows(1, 1)
                body(0, True, False)
                with act.Fori(1, TURNS - 1) as it:
                    body(it, False, False)
                body(TURNS - 1, False, True)
                part(NG - 1, GPT - 1, 0)
                copy_out(NG - 2, GPT - 2)
                part(NG - 1, GPT - 1, 1)
                copy_out(NG - 1, GPT - 1)

            edges(RA, COLS_A, ROW_A, NS, 12)
            root(stat[:, 3, :], 3, sqrt_out)
            edges(RB, COLS_B, ROW_B, TAB, 0)
            root(stat[:, 3, :], 4, sqrt_out)

        @block.vector
        def _(dve):
            tt, ts, red = dve.tensor_tensor, dve.tensor_scalar, dve.tensor_reduce

            def norm_relu(src_, dst_, tmp):
                m, rs = small[:, 0, :], small[:, 1, :]
                link(red(m, k16(src_), AX, ALU.add))
                link(ts(m, m, 1.0 / NS, None, ALU.mult))
                link(tt(k16(dst_), k16(src_), per_node(m, NS), ALU.subtract))
                link(tt(tmp, dst_, dst_, ALU.mult))
                link(red(rs, k16(tmp), AX, ALU.add))
                link(ts(rs, rs, 1.0 / NS, EPS, ALU.mult, ALU.add))
                dve_sqrt(rs)
                link(dve.reciprocal(rs, rs))
                link(tt(k16(dst_), k16(dst_), per_node(rs, NS), ALU.mult))
                return ts(dst_, dst_, 0.0, None, ALU.max)

            def split(src_, tmp, parts, w):
                p0, p1, p2 = (parts[:, :, q * w:(q + 1) * w] for q in range(3))
                link(dve.tensor_copy(p0, src_))
                link(tt(tmp, src_, p0, ALU.subtract))
                link(dve.tensor_copy(p1, tmp))
                link(tt(p2, tmp, p1, ALU.subtract))

            dve.memset(zero[:, :], 0.0).then_inc(zero_set, 1)
            dve.memset(ones[:, :], 1.0)
            link(dve.memset(stat[:, :, :], 0.0))
            dve.wait_ge(x_in, 16)
            dve.wait_ge(ld_const, 16 * NCONST)
            link(tt(Mk[:, :].rearrange("p (w b) -> p w b", b=NS), wl[:, :].unsqueeze(2).broadcast_to([P, NT * 8, NS]),
                    cmask[:, :].unsqueeze(1).broadcast_to([P, NT * 8, NS]), ALU.mult))
            link(dve.tensor_copy(bias_row.rearrange("p (w b) -> p w b", b=NS),
                                 bl[0:1, :].unsqueeze(2).broadcast_to([1, NT * 8, NS])))
            norm_relu(xs[:, :], h_p, d_p).then_inc(h0_done, 1)
            dve.memset(vmax[:, :], 2.0).then_inc(psem, 1)
            STEPS = 23
            g3 = lambda v_, c_: v_.rearrange("p (g t) -> p g t", t=c_)

            def make_piece(q, u, turn):
                b = pieces[u]
                step = [0]

                def pl(ins):
                    step[0] += 1
                    ins.then_inc(psem, 1)
                    dve.wait_ge(psem, STEPS * q + (step[0] + 1))

                wait_past(dve, pc_done, q)
                dve.wait_ge(pc_in[u], 112 * turn + 112)
                wait_past(dve, pc_out[u], 112 * turn)
                sv = g3(b.side, 4 * TPG)
                s0 = g3(b.side0, 2 * TPG)
                pl(tt(shp, b.vec, b.vec, ALU.mult))
                red(rootp, shp.rearrange("p (e c) -> p e c", c=SH), AX, ALU.add).then_inc(pc_sq, 1)
                pl(ts(t1p, b.src, float(N0 - 1), float(NT), ALU.min, ALU.mult))
                pl(ts(t2p, b.typ, 0.0, float(NT), ALU.is_equal, ALU.mult))
                pl(tt(t1p, t1p, t2p, ALU.add))
                pl(tt(t1p, t1p, b.typ, ALU.add))
                pl(ts(b.zi, t1p, -1.0, None, ALU.add))
                pl(dve.tensor_copy(sv[:, :, 24:32], g3(b.src, TPG)))
                pl(dve.tensor_copy(s0[:, :, 0:TPG], g3(b.dst, TPG)))
                pl(ts(t1p, b.dst, spare0[:, 0:1], None, ALU.subtract))
                pl(ts(t2p, b.dst, float(N0), None, ALU.is_lt))
                pl(tt(t1p, t1p, t2p, ALU.mult))
                pl(ts(s0[:, :, TPG:2 * TPG], g3(t1p, TPG), spare0[:, 0:1], None, ALU.add))
                pl(red(t1p[:, 0:PG], g3(t2p, TPG), AX, ALU.max))
                pl(tt(t1p[:, 0:PG], t1p[:, 0:PG], b.turn, ALU.mult))
                pl(red(t1p[:, PG:PG + 1], t1p[:, 0:PG], AX, ALU.max))
                lo, hi = b.stat[0:PG, 0:1], b.stat[0:PG, 1:2]
                pl(red(lo, b.drow[0:PG, :], AX, ALU.min))
                pl(red(hi, b.drow[0:PG, :], AX, ALU.max))
                pl(ts(lo, lo, float(NP - P), None, ALU.min))
                pl(dve.tensor_copy(b.first[0:PG, :], lo))
                pl(ts(b.wide[0:PG, :], hi, lo, float(P), ALU.subtract, ALU.is_ge))
                pl(ts(b.rel16[0:PG, :], b.drow[0:PG, :], lo, 255.0, ALU.subtract, ALU.min))
                pl(dve.tensor_copy(b.src16[0:PG, :], b.srow[0:PG, :]))
                dve.wait_ge(pc_root, q + 1)
                pl2 = ts(rootp, rootp, 1e-12, 3.0 ** -0.5, ALU.add, ALU.mult)
                pl(pl2)
                assert step[0] == STEPS, step
                dve.tensor_tensor(vmax[:, 0:1], vmax[:, 0:1], t1p[:, PG:PG + 1], ALU.max).then_inc(qsem, 1)
                dve.reciprocal(rootp, rootp).then_inc(qsem, 1)
                dve.wait_ge(qsem, 2 * q + 2)
                tt(sv[:, :, 0:24].rearrange("p g (t c) -> p g t c", c=SH),
                   b.vec.rearrange("p (g t c) -> p g t c", t=TPG, c=SH),
                   g3(rootp, TPG).unsqueeze(3).broadcast_to([P, PG, TPG, SH]), ALU.mult).then_inc(pc_done, 1)

            make_piece(0, 0, 0)
            make_piece(1, 1, 0)
            with dve.Fori(1, PIECES // 2) as h:
                for u in range(2):
                    make_piece(h * 2 + u, u, h)
            dve.wait_ge(pc_done, PIECES)
            dve.sem_inc(bound_in, 1)

            link(dve.memset(wide_sb[:, NG:NG + 2 * GPT], 0))
            dve.wait_ge(wide_in, 48)
            link(red(wide_turn[:, 0:1], wide_sb[:, 0:3], AX, ALU.max))
            red(wide_turn[:, 1:1 + TURNS], wide_sb[:, 3:3 + NG].rearrange("p (t s) -> p t s", s=GPT),
                AX, ALU.max).then_inc(wide_max, 1)
            link(red(any_wide[:, :], wide_sb[:, 0:NG], AX, ALU.max))
            link(ts(first0, first_i, float(NP0), None, ALU.min))

            for u in range(2):
                dve.wait_ge(pc_out[u], 112 * (PIECES // 2))
            R = R0
            dve.wait_ge(bound_out, 1)
            for s in range(GPT):
                last = dve.tensor_copy(zb[:, s, :, L0], code_sb[:, 0:1].broadcast_to([P, TPG]))
            last.then_inc(R.set_up, 1)
            dve.wait_ge(R.set_up, 1)
            dve.sem_inc(R.x_free, GPT)
            dve.sem_inc(R.inputs_free, GPT)
            turns = dve.value_load(last_turn_sb[0:1, 0:1], min_val=2, max_val=TURNS - 1) + 1

            def layer0_wide(it):
                for s in range(GPT):
                    g = it * GPT + s
                    dve.wait_ge(R.ld_rest[s], R.rest * it + R.rest)
                    for t in range(TPG):
                        last = ts(S0[:, s % 2, t * P:(t + 1) * P], rowb0[:, s, t * P:(t + 1) * P],
                                  sd0[:, s, t:t + 1], None, ALU.is_equal)
                    last.then_inc(R.S_built, 1)
                    ts(tmp0, sd0[:, s, TPG:2 * TPG], -1.0, spare0[:, 0:1], ALU.mult, ALU.add).then_inc(R.step, 1)
                    dve.wait_ge(R.out_ready, g + 1)
                    dve.wait_ge(R.out_free, g + 1)
                    dve.wait_ge(R.step, 3 * g + 1)
                    for b in range(3):
                        n = min(3, TPG - 3 * b)
                        last = dve.scalar_tensor_tensor(
                            out=tmp0[:, 3 * b:3 * b + n],
                            in0=banks[b][:, 0:n * (L0 + 1)].rearrange("p (t c) -> p t c", c=L0 + 1)[:, :, L0],
                            scalar=code_sb[:, 1:2], in1=tmp0[:, 3 * b:3 * b + n], op0=ALU.is_gt, op1=ALU.mult)
                    last.then_inc(R.step, 1)
                    dve.wait_ge(R.step, 3 * g + 2)
                    tt(ui0[:, s, :], tmp0, sd0[:, s, TPG:2 * TPG], ALU.add).then_inc(R.step, 1)
                    dve.wait_ge(R.step, 3 * g + 3)
                    dve.sem_inc(R.idx_ready, 1)
                    dve.sem_inc(R.x_free, 1)
                    dve.sem_inc(R.inputs_free, 1)

            def layer0_window(it):
                for s in range(GPT):
                    g = it * GPT + s
                    first = first0[:, bass.ds(g, 1)]
                    dve.wait_ge(R.ld_rest[s], 16 * it + 16)
                    tt(rel0, sd0[:, s, TPG:2 * TPG], first.broadcast_to([P, TPG]), ALU.subtract).then_inc(R.step, 1)
                    dve.wait_ge(R.out_free, g + 1)
                    tt(ui0[:, s, 0:1], first, spare0[:, 2:3], ALU.add).then_inc(R.idx_ready, 1)
                    dve.wait_ge(R.step, g + 1)
                    for t in range(TPG):
                        last = ts(S0[:, s % 2, t * P:(t + 1) * P], columns_sb, rel0[:, t:t + 1], None, ALU.is_equal)
                    last.then_inc(R.S_built, 1)
                    dve.wait_ge(R.joined, g + 1)
                    dve.wait_ge(R.S_built, g + 1)
                    dve.sem_inc(R.x_free, 1)
                    dve.sem_inc(R.inputs_free, 1)

            with dve.If(dve.value_load(any_wide[0:1, 0:1], min_val=0, max_val=1) > 0):
                with dve.Fori(0, turns) as it:
                    layer0_wide(it)
            with dve.Else():
                with dve.Fori(0, turns) as it:
                    layer0_window(it)

            dve.wait_ge(y_in, 16 * REPL)
            for r in range(REPL):
                link(tt(xs[:, :], xs[:, :], y_st[r], ALU.add))
            link(norm_relu(xs[:, :], nb[0], nb[1]))
            dve.sem_inc(h1_done, 1)
            split(k16(nb[0]), k16(nb[1]), hparts.rearrange("p (k c) -> p k c", c=3 * NS), NS)
            dve.sem_inc(h1_done, 1)
            dve.wait_ge(h1_out, 32)

            def edges(R, cols, I, J):
                M = Mflat[:, 0:2 * TPG * cols].rearrange("p (s t c) -> p s t c", s=2, t=TPG)
                round_a = cols == COLS_A
                live = LIVE[R.n - 1]

                def sh_of(s):
                    return sd[:, s, 0:24].rearrange("p (t c) -> p t c", c=SH).unsqueeze(2).broadcast_to([P, TPG, NV, SH])

                def build_G(g, s, turn):
                    dve.wait_ge(R.ld_rest[s], R.rest * turn + R.rest)
                    wait_past(dve, R.picked, g - 1)
                    ts(G[:, s % 2, :], drow16[:, s, :], spare0[:, 2:3], None, ALU.is_equal).then_inc(R.G_built, 1)

                Mp = Mparts[:, 0:3 * TPG * cols].rearrange("p (q t c) -> p q t c", q=3, t=TPG)

                def prepare(g, s):
                    if not round_a:
                        dve.wait_ge(R.x_ready, g + 1)
                        tt(vtmp, xg[:, s, :, 0:NV * SH].rearrange("p t (j c) -> p t j c", c=SH), sh_of(s),
                           ALU.mult).then_inc(R.vec, 1)
                    dve.tensor_copy(home[:, s, :], sd[:, s, 24:32])
                    ts(away[:, s, :], sd[:, s, 24:32], -1.0, spare0[:, 1:2], ALU.mult, ALU.add).then_inc(R.step, 1)
                    if not round_a:
                        dve.wait_ge(R.vec, 2 * g + 1)
                        red(xg[:, s, :, 28:32], vtmp, AX, ALU.add).then_inc(R.vec, 1)
                        dve.wait_ge(R.vec, 2 * g + 2)

                def multiply(g, s, k, first):
                    if k == 0 and round_a:
                        dve.wait_ge(R.x_ready, g + 1)
                    dve.wait_ge(R.weights, 4 * g + k + 1)
                    if not (first and k < 2):
                        dve.wait_ge(R.red, 4 * g + k - 1)
                    tt(prod[:, k % 2].rearrange("p t (j i) -> p t j i", i=I),
                       wide[k % 2][:, :, 0:WN].rearrange("p t (j i) -> p t j i", i=I),
                       xg[:, s, k:TPG:4, 12:12 + I].unsqueeze(2).broadcast_to([P, 2, J, I]),
                       ALU.mult).then_inc(R.prod, 1)

                def reduce_(g, s, k):
                    dve.wait_ge(R.prod, 4 * g + k + 1)
                    red(M[:, s % 2, k:TPG:4, 0:J], prod[:, k % 2].rearrange("p t (j i) -> p t j i", i=I),
                        AX, ALU.add).then_inc(R.red, 1)

                def rest(g, s):
                    dve.wait_ge(R.cast, 2 * g + 1)
                    Ms = M[:, s % 2, :, 0:live]
                    tt(Ms, Ms, Mp[:, 0, :, 0:live], ALU.subtract).then_inc(R.rest_left, 1)

                def last_part(g, s):
                    dve.wait_ge(R.cast, 2 * g + 2)
                    tt(Mp[:, 2, :, 0:live], M[:, s % 2, :, 0:live], Mp[:, 1, :, 0:live],
                       ALU.subtract).then_inc(R.parted, 1)

                def targets(g, s):
                    dve.wait_ge(R.out_ready, g + 1)
                    dve.wait_ge(R.out_free, g + 1)
                    ps = banks[2 + s % 2][:, 0:TPG * cols].rearrange("p (t c) -> p t c", c=cols)
                    dve.scalar_tensor_tensor(out=away[:, s, :], in0=ps[:, :, cols - 1], scalar=code_sb[:, 1:2],
                                             in1=away[:, s, :], op0=ALU.is_gt, op1=ALU.mult).then_inc(R.hop, 1)
                    dve.wait_ge(R.hop, g + 1)
                    tt(ui[:, s, :], away[:, s, :], home[:, s, :], ALU.add).then_inc(R.idx_ready, 1)

                def body(it, first, last):
                    for s in range(GPT):
                        g = it * GPT + s
                        f = first and s == 0
                        before = (s - 1) % GPT
                        if not (last and s + 2 >= GPT):
                            build_G(g + 2, (s + 2) % GPT, it + (s + 2) // GPT)
                        prepare(g, s)
                        multiply(g, s, 0, f)
                        if not f:
                            rest(g - 1, before)
                        multiply(g, s, 1, f)
                        reduce_(g, s, 0)
                        if not (first and s < 2):
                            targets(g - 2, (s - 2) % GPT)
                        multiply(g, s, 2, f)
                        reduce_(g, s, 1)
                        if not f:
                            last_part(g - 1, before)
                        multiply(g, s, 3, f)
                        reduce_(g, s, 2)
                        reduce_(g, s, 3)
                        dve.wait_ge(R.red, 4 * g + 4)
                        dve.sem_inc(R.x_free, 1)
                        if round_a:
                            tt(M[:, s % 2, :, 20:32].rearrange("p t (j c) -> p t j c", c=SH),
                               M[:, s % 2, :, 16:20].unsqueeze(3).broadcast_to([P, TPG, NV, SH]), sh_of(s),
                               ALU.mult).then_inc(R.msgs, 1)
                            dve.wait_ge(R.msgs, g + 1)
                        else:
                            dve.sem_inc(R.msgs, 1)
                        dve.sem_inc(R.inputs_free, 1)

                last = dve.memset(ea, 0.0)
                last = dve.memset(Mflat, 1.0)
                last = dve.memset(outflat, 0.0)
                link(last)
                for b in range(2):
                    last = dve.tensor_copy(M[:, b, :, cols - 1], code_sb[:, 0:1].broadcast_to([P, TPG]))
                link(last)
                dve.sem_inc(R.set_up, 1)
                dve.sem_inc(R.x_free, GPT)
                dve.sem_inc(R.inputs_free, GPT)
                build_G(0, 0, 0)
                build_G(1, 1, 0)
                body(0, True, False)
                with dve.Fori(1, TURNS - 1) as it:
                    body(it, False, False)
                body(TURNS - 1, False, True)
                rest(NG - 1, GPT - 1)
                targets(NG - 2, GPT - 2)
                last_part(NG - 1, GPT - 1)
                targets(NG - 1, GPT - 1)

            def add_up(n, st, dst_of, row):
                for q in range(TP):
                    dve.wait_ge(t_in[n], 16 * REPL * (q + 1))
                    for r in range(1, REPL):
                        link(tt(st[0], st[0], st[r], ALU.add))
                    dst_of(q, st[0].rearrange("p (k c) -> p k c", c=row))
                    dve.sem_inc(t_used[n], 1)

            edges(RA, COLS_A, NS, NS + NV)

            Tk = T[:, :].rearrange("p (k c) -> p k c", c=TAB)
            pn = [0]

            def piece_a(q, s_):
                ks = slice(q * KP, (q + 1) * KP)
                rc = rcount[:, ks]
                link(ts(rc, s_[:, :, 28], 1.0, None, ALU.max))
                link(dve.reciprocal(rc, rc))
                link(tt(rc, rc, mask[:, ks], ALU.mult))
                rw = lambda w: rc.unsqueeze(2).broadcast_to([P, KP, w])
                link(tt(Tk[:, ks, 0:12], s_[:, :, NS:NS + 12], rw(12), ALU.mult))
                link(tt(Tk[:, ks, 12:28], s_[:, :, 0:NS], rw(NS), ALU.mult))

            def total(src_, w):
                link(red(stat[:, 0, 0:w], src_.rearrange("p k c -> p c k"), AX, ALU.add))
                dve.sem_inc(part_in, 1)
                pn[0] += 1
                dve.wait_ge(part_sum, pn[0])

            def batch_norm(V, w, first_s, gs, bs, gv):
                sq = sqT[:, 0:K * w].rearrange("p (k c) -> p k c", c=w)
                mean, var, scale = stat[:, 1, 0:w], stat[:, 2, 0:w], stat[:, 3, 0:w]
                S_ = slice(first_s, first_s + NS)
                total(V, w)
                link(ts(mean, banks[0][:, 0:w], 1.0 / N, None, ALU.mult))
                if first_s:
                    link(dve.memset(stat[:, 1, 0:first_s], 0.0))
                link(tt(V, V, per_chan(mean, w), ALU.subtract))
                link(tt(sq, V, V, ALU.mult))
                link(tt(sq, sq, per_node(mask[:, :], w), ALU.mult))
                total(sq, w)
                link(ts(var, banks[0][:, 0:w], 1.0 / N, None, ALU.mult))
                if first_s:
                    link(red(stat[:, 4, 0:NV], stat[:, 2, 0:12].rearrange("p (j c) -> p j c", c=SH), AX, ALU.add))
                    link(ts(stat[:, 4, 0:NV], stat[:, 4, 0:NV], 1.0 / SH, None, ALU.mult))
                    link(dve.tensor_copy(stat[:, 2, 0:12].rearrange("p (j c) -> p j c", c=SH),
                                         stat[:, 4, 0:NV].unsqueeze(2).broadcast_to([P, NV, SH])))
                link(ts(scale, var, EPS, None, ALU.add))
                dve_sqrt(scale)
                link(dve.reciprocal(scale, scale))
                link(tt(stat[:, 3, S_], stat[:, 3, S_], gs, ALU.mult))
                if first_s:
                    link(tt(stat[:, 3, 0:12].rearrange("p (j c) -> p j c", c=SH),
                            stat[:, 3, 0:12].rearrange("p (j c) -> p j c", c=SH),
                            gv.unsqueeze(2).broadcast_to([P, NV, SH]), ALU.mult))
                    link(ts(stat[:, 3, 0:12], stat[:, 3, 0:12], 3.0 ** -0.5, None, ALU.mult))
                link(tt(V, V, per_chan(scale, w), ALU.mult))
                link(tt(V[:, :, S_], V[:, :, S_], per_chan(bs, NS), ALU.add))

            add_up(0, stA, piece_a, ROW_A)
            link(ts(T[:, :], T[:, :], NS ** -0.5, None, ALU.mult))
            batch_norm(Tk, TAB, 12, bn[:, 0:NS], bn[:, NS:2 * NS], bn[:, 4 * NS:4 * NS + NV])
            dve.sem_inc(s_done, 1)
            split(Tk, sqT.rearrange("p (k c) -> p k c", c=TAB), sparts.rearrange("p (k c) -> p k c", c=3 * TAB), TAB)
            dve.sem_inc(s_done, 1)
            dve.wait_ge(s_out, 32)

            edges(RB, COLS_B, NS + NV, NS)
            Vb = T[:, 0:XW].rearrange("p (k c) -> p k c", c=NS)

            def piece_b(q, s_):
                ks = slice(q * KP, (q + 1) * KP)
                link(tt(Vb[:, ks, :], s_, rcount[:, ks].unsqueeze(2).broadcast_to([P, KP, NS]), ALU.mult))

            add_up(1, stB, piece_b, ROW_B)
            link(ts(T[:, 0:XW], T[:, 0:XW], (NS + NV) ** -0.5, None, ALU.mult))
            batch_norm(Vb, NS, 0, bn[:, 2 * NS:3 * NS], bn[:, 3 * NS:4 * NS], None)
            link(tt(xs[:, :], xs[:, :], T[:, 0:XW], ALU.add))
            dve.sem_inc(fin, 1)


NCONST = 18


def lay_out(i):
    f = np.float32
    a = {k: np.asarray(v) for k, v in i.items()}
    N, E = a["x"].shape[0], a["src"].shape[0]
    K = -(-N // (P * 8)) * 8
    NP = P * K
    step = EPG * PIECES
    EP = -(-E // step) * step
    NG = EP // EPG
    pad = EP - E

    def fill(v, value):
        return np.concatenate([v, np.full((pad,) + v.shape[1:], value, v.dtype)])

    src, dst, typ = fill(a["src"], N), fill(a["dst"], N - 1), fill(a["edge_type_6"], 1)
    if NP == N:
        raise ValueError("needs a padded node")
    cols = lambda v: np.ascontiguousarray(v.reshape(EP // P, P).T)
    vec = fill(a["edge_attr_3"], 0)
    w_t = a["L0_gnn_W"].transpose(2, 0, 1).reshape(8, NT * 8)

    def second(w, b, vec_major):
        w = np.concatenate([w, b[None]])
        wa = w[:, :NS * NS].reshape(-1, NS, NS)
        if vec_major:
            wb = w[:, NS * NS:].reshape(-1, NV, NS)
            full = np.concatenate([wa, wb], 1)
        else:
            wb = w[:, NS * NS:].reshape(-1, NS, NV)
            full = np.concatenate([wa, wb], 2)
        return np.ascontiguousarray(full.transpose(0, 2, 1).reshape(-1, WN))

    def twice(w, rows, columns):
        w = np.pad(w, ((0, rows), (0, columns)))
        z = np.zeros_like(w)
        return np.concatenate([np.concatenate([w, z], 1), np.concatenate([z, w], 1)])

    p = np.arange(P)
    arr = {
        "x": np.concatenate([a["x"], np.zeros((NP - N, NS), f)]).reshape(P, K * NS),
        "src_cols": cols(src), "dst_cols": cols(dst), "typ_cols": cols(typ),
        "vec_cols": np.ascontiguousarray(vec.reshape(EP // P, P, 3).transpose(1, 0, 2).reshape(P, -1)),
        "src_row": src, "dst_row": dst,
        "attr": np.ascontiguousarray(fill(a["edge_attr_48"], 0).T),
        "turn_no": np.tile((np.arange(NG) // GPT).astype(f), (P, 1)),
        "ident": np.eye(P, dtype=f),
        "code": np.stack([3.0 ** (64 - p), 2 * 3.0 ** (64 - p)], 1).astype(f),
        "spare": np.stack([NP // 8 + p, NP + p, p], 1).astype(f),
        "columns": np.tile(p.astype(f), (P, 1)),
        "node_mask": (np.arange(NP) < N).astype(f).reshape(P, K),
        "copy_mask": (p[:, None] % NS == np.arange(NS)[None]).astype(f),
        "w_l0": np.repeat(w_t, NS, axis=0),
        "b_l0": a["L0_gnn_Bv"].reshape(-1),
        "w1": np.stack([twice(a[f"L1_gnn_fc{r}_w1"], 64 - H, 64 - H) for r in (0, 1)]),
        "b1": np.stack([np.tile(np.concatenate([a[f"L1_gnn_fc{r}_b1"], np.ones(1, f), np.zeros(63 - H, f)]), 2)
                        for r in (0, 1)])[:, :, None],
        "w2a": twice(second(a["L1_gnn_fc0_w2"], a["L1_gnn_fc0_b2"], False), 63 - H, 0),
        "w2b": twice(second(a["L1_gnn_fc1_w2"], a["L1_gnn_fc1_b2"], True), 63 - H, 0),
        "gs0": a["L1_gnn_bn0_gs"], "bs0": a["L1_gnn_bn0_bs"], "gv0": a["L1_gnn_bn0_gv"],
        "gs1": a["L1_gnn_bn1_gs"], "bs1": a["L1_gnn_bn1_bs"],
    }
    return {k: np.ascontiguousarray(v) for k, v in arr.items()}, N, NG, K


def kernel(**inputs):
    import concourse.bacc as bacc
    from concourse.bass_utils import run_bass_kernel_spmd

    arrays, N, NG, K = lay_out(inputs)
    nc = bacc.Bacc("TRN2", target_bir_lowering=False, num_devices=1)
    aps = {k: nc.dram_tensor("in_" + k, v.shape, mybir.dt.from_np(v.dtype), kind="ExternalInput").ap()
           for k, v in arrays.items()}
    out = nc.dram_tensor("out_x", (P, K * NS), F32, kind="ExternalOutput").ap()
    build(nc, N, NG, out=out, **aps)
    r = run_bass_kernel_spmd(nc, [{"in_" + k: v for k, v in arrays.items()}], core_ids=[0])
    return r.results[0]["out_x"].reshape(P * K, NS)[:N]
```
